# Optimizing a Trainium2 kernel written in Bass

```python
import numpy as np
import jax
import jax.numpy as jnp

def _softmax(x, axis=-1):
    return jax.nn.softmax(x, axis=axis)

def _gelu(x):
    return jax.nn.gelu(x, approximate=True)

def _silu(x):
    return jax.nn.silu(x)

def _sigmoid(x):
    return jax.nn.sigmoid(x)

def _layernorm(x, axis=-1, eps=1e-05):
    m = jnp.mean(x, axis=axis, keepdims=True)
    v = jnp.var(x, axis=axis, keepdims=True)
    return (x - m) / jnp.sqrt(v + eps)

def _scatter_add(tgt, idx, src, axis=0):
    return tgt.at[idx].add(src)

def _segment_sum(src, seg, n):
    return jax.ops.segment_sum(src, seg, n)
kernel_name = 'mk_xattn_ffn_d1_seqx_r4_190d19'

def setup_inputs(seed: int=0):
    np.random.seed(seed)
    _w = jnp.asarray

    def _rec_inputs():
        import jax
        import jax.numpy as jnp
        _rk = jax.random.key(seed)
        x = -0.0001231 + 1 * jax.random.normal(jax.random.fold_in(_rk, 1), (16, 256, 256), jnp.float32)
        _lenS = 256 - jax.random.randint(jax.random.fold_in(_rk, 7), (16,), 0, max(1, 256 // 4) + 1, jnp.int32)
        _lenS2 = 256 - jax.random.randint(jax.random.fold_in(_rk, 8), (16,), 0, max(1, 256 // 4) + 1, jnp.int32)
        _ctx_1024P = jax.random.normal(jax.random.fold_in(_rk, 11), (16, 16, 256), jnp.float32)
        _ctx_1024c = jax.random.dirichlet(jax.random.fold_in(_rk, 511), 0.3 * jnp.ones((16,), jnp.float32), (16, 256))
        _ctx_1024t = jnp.einsum('bsk,bkd->bsd', _ctx_1024c, _ctx_1024P)
        _ctx_1024t = _ctx_1024t * jax.lax.rsqrt(jnp.mean(jnp.square(_ctx_1024t)) + 1e-12) * 0.953939
        ctx_1024 = -0.000137203 + 0.999727 * (_ctx_1024t + 0.3 * jax.random.normal(jax.random.fold_in(_rk, 611), (16, 256, 256), jnp.float32))
        return (x, ctx_1024)
    x, ctx_1024 = _rec_inputs()

    def _L0_xattn_setup():
        import jax, jax.numpy as jnp
        import numpy as np
        B, Q, K, D = (4, 375, 375, 256)
        H, HD = (16, 64)
        key = jax.random.key(seed)
        ks = jax.random.split(key, 10)
        s = 0.02
        return {'inputs_q': jax.random.normal(ks[0], (B, Q, D), jnp.float32), 'inputs_kv': jax.random.normal(ks[1], (B, K, D), jnp.float32), 'Wq': jax.random.normal(ks[2], (D, H, HD), jnp.float32) * s, 'bq': jnp.zeros((H, HD), jnp.float32), 'Wk': jax.random.normal(ks[3], (D, H, HD), jnp.float32) * s, 'bk': jnp.zeros((H, HD), jnp.float32), 'Wv': jax.random.normal(ks[4], (D, H, HD), jnp.float32) * s, 'bv': jnp.zeros((H, HD), jnp.float32), 'Wo': jax.random.normal(ks[5], (H, HD, D), jnp.float32) * s, 'bo': jnp.zeros((D,), jnp.float32)}
    _L0_xattn_all = _L0_xattn_setup()
    _L0_xattn_in = {k: v for k, v in _L0_xattn_all.items() if k in ('Wq', 'bq', 'Wk', 'bk', 'Wv', 'bv', 'Wo', 'bo')}
    del _L0_xattn_all

    def _L0_ffn_setup():
        import jax, jax.numpy as jnp
        import numpy as np
        D_MODEL = 256
        N_HEADS = 16
        HEAD_DIM = D_MODEL // N_HEADS
        FFN_DIM = 1024
        N_EXPERTS = 8
        CAP_FRAC = 0.25
        MOE_TOKEN_DROPOUT = 0.2
        LN_EPS = 1e-05
        B, S = (4, 128)

        def _layer_norm(x, g, b):
            mu = x.mean(-1, keepdims=True)
            var = ((x - mu) ** 2).mean(-1, keepdims=True)
            return (x - mu) * jax.lax.rsqrt(var + LN_EPS) * g + b

        def _self_attention(x, wq, bq, wk, bk, wv, bv, wo, bo):
            b, s, d = x.shape
            q = ((x @ wq + bq) * HEAD_DIM ** (-0.5)).reshape(b, s, N_HEADS, HEAD_DIM)
            k = (x @ wk + bk).reshape(b, s, N_HEADS, HEAD_DIM)
            v = (x @ wv + bv).reshape(b, s, N_HEADS, HEAD_DIM)
            scores = jnp.einsum('bqhd,bkhd->bhqk', q, k)
            p = jax.nn.softmax(scores, axis=-1)
            o = jnp.einsum('bhqk,bkhd->bqhd', p, v).reshape(b, s, d)
            return o @ wo + bo

        def _moe_ffn(x, wr, w1, b1, w2, b2):
            T, D = x.shape
            C = int(np.ceil(CAP_FRAC * T))
            logits = x @ wr
            probs = jax.nn.softmax(logits, axis=-1)
            top1 = jnp.argmax(probs, axis=-1)
            m1 = jax.nn.one_hot(top1, N_EXPERTS, dtype=x.dtype)
            top2 = jnp.argmax(jnp.where(m1 > 0, -jnp.inf, logits), axis=-1)
            m2 = jax.nn.one_hot(top2, N_EXPERTS, dtype=x.dtype)
            loc1 = jnp.cumsum(m1, axis=0) - 1.0
            loc2 = jnp.cumsum(m2, axis=0) - 1.0 + m1.sum(0, keepdims=True)
            m1 = m1 * (loc1 < C)
            m2 = m2 * (loc2 < C)
            t1 = (probs * m1).sum(-1)
            t2 = (probs * m2).sum(-1)
            denom = jnp.maximum(t1 + t2, jnp.finfo(x.dtype).eps)
            t1, t2 = (t1 / denom, t2 / denom)
            tok = jnp.arange(T)
            s1 = loc1[tok, top1].astype(jnp.int32)
            s2 = loc2[tok, top2].astype(jnp.int32)
            v1 = m1[tok, top1] > 0
            v2 = m2[tok, top2] > 0
            s1 = jnp.where(v1, s1, C)
            s2 = jnp.where(v2, s2, C)
            buf = jnp.zeros((N_EXPERTS, C, D), x.dtype)
            buf = buf.at[top1, s1].set(x, mode='drop')
            buf = buf.at[top2, s2].set(x, mode='drop')
            h = jax.nn.relu(jnp.einsum('ecd,edf->ecf', buf, w1) + b1[:, None, :])
            y = (jnp.einsum('ecf,efd->ecd', h, w2) + b2[:, None, :]) * (1.0 - MOE_TOKEN_DROPOUT)
            y1 = y[top1, jnp.minimum(s1, C - 1)]
            y2 = y[top2, jnp.minimum(s2, C - 1)]
            g1 = t1 * v1
            g2 = t2 * v2
            return g1[:, None] * y1 + g2[:, None] * y2
        key = jax.random.key(seed)
        ks = jax.random.split(key, 20)

        def w(k, shape, scale=0.02):
            return jax.random.normal(k, shape, jnp.float32) * scale
        return {'x': jax.random.normal(ks[0], (B, S, D_MODEL), jnp.float32), 'wq': w(ks[1], (D_MODEL, D_MODEL)), 'bq': w(ks[2], (D_MODEL,)), 'wk': w(ks[3], (D_MODEL, D_MODEL)), 'bk': w(ks[4], (D_MODEL,)), 'wv': w(ks[5], (D_MODEL, D_MODEL)), 'bv': w(ks[6], (D_MODEL,)), 'wo': w(ks[7], (D_MODEL, D_MODEL)), 'bo': w(ks[8], (D_MODEL,)), 'ln1_g': 1.0 + w(ks[9], (D_MODEL,)), 'ln1_b': w(ks[10], (D_MODEL,)), 'ln2_g': 1.0 + w(ks[11], (D_MODEL,)), 'ln2_b': w(ks[12], (D_MODEL,)), 'wr': w(ks[13], (D_MODEL, N_EXPERTS)), 'w1': w(ks[14], (N_EXPERTS, D_MODEL, FFN_DIM)), 'b1': w(ks[15], (N_EXPERTS, FFN_DIM)), 'w2': w(ks[16], (N_EXPERTS, FFN_DIM, D_MODEL)), 'b2': w(ks[17], (N_EXPERTS, D_MODEL))}
    _L0_ffn_all = _L0_ffn_setup()
    _L0_ffn_in = {k: v for k, v in _L0_ffn_all.items() if k in ('wq', 'bq', 'wk', 'bk', 'wv', 'bv', 'wo', 'bo', 'ln1_g', 'ln1_b', 'ln2_g', 'ln2_b', 'wr', 'w1', 'b1', 'w2', 'b2')}
    del _L0_ffn_all
    return {'x': x, 'ctx_1024': ctx_1024, 'L0_xattn_Wq': _L0_xattn_in['Wq'], 'L0_xattn_bq': _L0_xattn_in['bq'], 'L0_xattn_Wk': _L0_xattn_in['Wk'], 'L0_xattn_bk': _L0_xattn_in['bk'], 'L0_xattn_Wv': _L0_xattn_in['Wv'], 'L0_xattn_bv': _L0_xattn_in['bv'], 'L0_xattn_Wo': _L0_xattn_in['Wo'], 'L0_xattn_bo': _L0_xattn_in['bo'], 'L0_ffn_wq': _L0_ffn_in['wq'], 'L0_ffn_bq': _L0_ffn_in['bq'], 'L0_ffn_wk': _L0_ffn_in['wk'], 'L0_ffn_bk': _L0_ffn_in['bk'], 'L0_ffn_wv': _L0_ffn_in['wv'], 'L0_ffn_bv': _L0_ffn_in['bv'], 'L0_ffn_wo': _L0_ffn_in['wo'], 'L0_ffn_bo': _L0_ffn_in['bo'], 'L0_ffn_ln1_g': _L0_ffn_in['ln1_g'], 'L0_ffn_ln1_b': _L0_ffn_in['ln1_b'], 'L0_ffn_ln2_g': _L0_ffn_in['ln2_g'], 'L0_ffn_ln2_b': _L0_ffn_in['ln2_b'], 'L0_ffn_wr': _L0_ffn_in['wr'], 'L0_ffn_w1': _L0_ffn_in['w1'], 'L0_ffn_b1': _L0_ffn_in['b1'], 'L0_ffn_w2': _L0_ffn_in['w2'], 'L0_ffn_b2': _L0_ffn_in['b2']}

def reference(x, ctx_1024, L0_xattn_Wq, L0_xattn_bq, L0_xattn_Wk, L0_xattn_bk, L0_xattn_Wv, L0_xattn_bv, L0_xattn_Wo, L0_xattn_bo, L0_ffn_wq, L0_ffn_bq, L0_ffn_wk, L0_ffn_bk, L0_ffn_wv, L0_ffn_bv, L0_ffn_wo, L0_ffn_bo, L0_ffn_ln1_g, L0_ffn_ln1_b, L0_ffn_ln2_g, L0_ffn_ln2_b, L0_ffn_wr, L0_ffn_w1, L0_ffn_b1, L0_ffn_w2, L0_ffn_b2):
    import jax
    import jax.numpy as jnp

    def _L0_xattn_ref(inputs_q, inputs_kv, Wq, bq, Wk, bk, Wv, bv, Wo, bo):
        import jax, jax.numpy as jnp
        import numpy as np
        B, Q, K, D = (4, 375, 375, 256)
        H, HD = (16, 64)
        q = jnp.einsum('bqm,mhd->bqhd', inputs_q, Wq) + bq
        k = jnp.einsum('bkm,mhd->bkhd', inputs_kv, Wk) + bk
        v = jnp.einsum('bkm,mhd->bkhd', inputs_kv, Wv) + bv
        q = q / jnp.sqrt(jnp.asarray(HD, q.dtype))
        attn = jnp.einsum('bqhd,bkhd->bhqk', q, k)
        attn = jax.nn.softmax(attn, axis=-1)
        out = jnp.einsum('bhqk,bkhd->bqhd', attn, v)
        return jnp.einsum('bqhd,hdm->bqm', out, Wo) + bo

    def _L0_ffn_ref(x, wq, bq, wk, bk, wv, bv, wo, bo, ln1_g, ln1_b, ln2_g, ln2_b, wr, w1, b1, w2, b2):
        import jax, jax.numpy as jnp
        import numpy as np
        D_MODEL = 256
        N_HEADS = 16
        HEAD_DIM = D_MODEL // N_HEADS
        FFN_DIM = 1024
        N_EXPERTS = 8
        CAP_FRAC = 0.25
        MOE_TOKEN_DROPOUT = 0.2
        LN_EPS = 1e-05
        B, S = (4, 128)

        def _layer_norm(x, g, b):
            mu = x.mean(-1, keepdims=True)
            var = ((x - mu) ** 2).mean(-1, keepdims=True)
            return (x - mu) * jax.lax.rsqrt(var + LN_EPS) * g + b

        def _self_attention(x, wq, bq, wk, bk, wv, bv, wo, bo):
            b, s, d = x.shape
            q = ((x @ wq + bq) * HEAD_DIM ** (-0.5)).reshape(b, s, N_HEADS, HEAD_DIM)
            k = (x @ wk + bk).reshape(b, s, N_HEADS, HEAD_DIM)
            v = (x @ wv + bv).reshape(b, s, N_HEADS, HEAD_DIM)
            scores = jnp.einsum('bqhd,bkhd->bhqk', q, k)
            p = jax.nn.softmax(scores, axis=-1)
            o = jnp.einsum('bhqk,bkhd->bqhd', p, v).reshape(b, s, d)
            return o @ wo + bo

        def _moe_ffn(x, wr, w1, b1, w2, b2):
            T, D = x.shape
            C = int(np.ceil(CAP_FRAC * T))
            logits = x @ wr
            probs = jax.nn.softmax(logits, axis=-1)
            top1 = jnp.argmax(probs, axis=-1)
            m1 = jax.nn.one_hot(top1, N_EXPERTS, dtype=x.dtype)
            top2 = jnp.argmax(jnp.where(m1 > 0, -jnp.inf, logits), axis=-1)
            m2 = jax.nn.one_hot(top2, N_EXPERTS, dtype=x.dtype)
            loc1 = jnp.cumsum(m1, axis=0) - 1.0
            loc2 = jnp.cumsum(m2, axis=0) - 1.0 + m1.sum(0, keepdims=True)
            m1 = m1 * (loc1 < C)
            m2 = m2 * (loc2 < C)
            t1 = (probs * m1).sum(-1)
            t2 = (probs * m2).sum(-1)
            denom = jnp.maximum(t1 + t2, jnp.finfo(x.dtype).eps)
            t1, t2 = (t1 / denom, t2 / denom)
            tok = jnp.arange(T)
            s1 = loc1[tok, top1].astype(jnp.int32)
            s2 = loc2[tok, top2].astype(jnp.int32)
            v1 = m1[tok, top1] > 0
            v2 = m2[tok, top2] > 0
            s1 = jnp.where(v1, s1, C)
            s2 = jnp.where(v2, s2, C)
            buf = jnp.zeros((N_EXPERTS, C, D), x.dtype)
            buf = buf.at[top1, s1].set(x, mode='drop')
            buf = buf.at[top2, s2].set(x, mode='drop')
            h = jax.nn.relu(jnp.einsum('ecd,edf->ecf', buf, w1) + b1[:, None, :])
            y = (jnp.einsum('ecf,efd->ecd', h, w2) + b2[:, None, :]) * (1.0 - MOE_TOKEN_DROPOUT)
            y1 = y[top1, jnp.minimum(s1, C - 1)]
            y2 = y[top2, jnp.minimum(s2, C - 1)]
            g1 = t1 * v1
            g2 = t2 * v2
            return g1[:, None] * y1 + g2[:, None] * y2
        h = _layer_norm(x, ln1_g, ln1_b)
        h = _self_attention(h, wq, bq, wk, bk, wv, bv, wo, bo)
        x = x + h
        h = _layer_norm(x, ln2_g, ln2_b)
        b, s, d = h.shape
        moe = _moe_ffn(h.reshape(b * s, d), wr, w1, b1, w2, b2).reshape(b, s, d)
        return x + moe
    x = x + _L0_xattn_ref(_layernorm(x, axis=-1), ctx_1024, L0_xattn_Wq, L0_xattn_bq, L0_xattn_Wk, L0_xattn_bk, L0_xattn_Wv, L0_xattn_bv, L0_xattn_Wo, L0_xattn_bo)
    x = x + _L0_ffn_ref(_layernorm(x, axis=-1), L0_ffn_wq, L0_ffn_bq, L0_ffn_wk, L0_ffn_bk, L0_ffn_wv, L0_ffn_bv, L0_ffn_wo, L0_ffn_bo, L0_ffn_ln1_g, L0_ffn_ln1_b, L0_ffn_ln2_g, L0_ffn_ln2_b, L0_ffn_wr, L0_ffn_w1, L0_ffn_b1, L0_ffn_w2, L0_ffn_b2)
    return x

_drawn_inputs = setup_inputs


def setup_inputs(seed=0):
    import zlib

    import numpy as np

    out = dict(_drawn_inputs(seed))
    spreads = {'L0_xattn_bq': (0.0, 0.8),
     'L0_xattn_bk': (0.0, 2.0),
     'L0_xattn_bv': (0.0, 0.1),
     'L0_xattn_bo': (0.0, 0.1)}
    factors = {'L0_xattn_Wq': 8.0,
     'L0_xattn_Wk': 8.0,
     'L0_ffn_wq': 8.0,
     'L0_ffn_bq': 8.0,
     'L0_ffn_wk': 8.0,
     'L0_ffn_bk': 200.0,
     'L0_ffn_wv': 5.685,
     'L0_ffn_bv': 38.775,
     'L0_ffn_wo': 5.185,
     'L0_ffn_bo': 38.088,
     'L0_ffn_ln1_g': 8.0,
     'L0_ffn_ln1_b': 8.0,
     'L0_ffn_ln2_g': 64.0,
     'L0_ffn_ln2_b': 64.0,
     'L0_ffn_b1': 200.0,
     'L0_ffn_b2': 64.0}
    for name, (base, spread) in spreads.items():
        noise = np.random.default_rng([zlib.crc32(name.encode()), seed]).standard_normal(out[name].shape)
        drawn = base * np.exp(spread * noise) if base else spread * noise
        out[name] = jnp.asarray(drawn.astype(out[name].dtype))
    for name, factor in factors.items():
        out[name] = (out[name] * factor).astype(out[name].dtype)
    return out
```

```python
from contextlib import ExitStack

import concourse.bass as bass
from concourse import mybir

F32 = mybir.dt.float32
F32R = mybir.dt.float32r
BF16 = mybir.dt.bfloat16
I32 = mybir.dt.int32
U32 = mybir.dt.uint32
ALU = mybir.AluOpType
ACT = mybir.ActivationFunctionType
AX_X = mybir.AxisListType.X

P = 128
EPS = 1e-5
FLT_EPS = 1.1920928955078125e-07
FAR = 1048576.0


def xattn_moe(nc, x, ctx, Wq, bq, Wk, bk, Wv, bv, Wo, bo, swq, sbq, swk, sbk, swv, sbv, swo, sbo,
              g1, b1n, g2, b2n, wr, w1, b1, w2, b2, out):
    B, S, D = x.shape
    _, H, HD = Wq.shape
    E, _, F = w1.shape
    T = B * S
    C = -(-T // 4)
    KD, TT = D // P, S // P
    HT = H * HD // P
    SD = D // H
    ST = H // 4
    GX, GY = H // 2, 2
    FT = F // P
    XS, YS = float(HD) ** -0.5, float(SD) ** -0.5
    KEEP = 0.8
    assert S == 256 and D == 256 and HD == 64 and SD == 16 and H == 16 and E == 8 and C == 1024

    base_d = nc.dram_tensor("base_rows", (T, D), F32).ap()
    n2_d = nc.dram_tensor("n2_rows", (T, D), F32).ap()
    y_d = nc.dram_tensor("y_rows", (E * C, D), F32).ap()
    route_d = nc.dram_tensor("route_rows", (B, P, TT * 16), F32).ap()
    slot_d = [nc.dram_tensor(f"slot_tokens_{j}", (E * C, 1), I32).ap() for j in range(2)]

    whole = ExitStack()
    with whole:
        def sem(name):
            return whole.enter_context(nc.semaphore(name))

        def psum(name):
            return whole.enter_context(nc.psum_tensor(name, [P, 512], F32))

        def keep(name, shape, dt=F32):
            return whole.enter_context(nc.sbuf_tensor(name, shape, dt))

        Sp = [psum(f"scoresT{k}") for k in range(2)]
        Sn = [psum(f"scores{k}") for k in range(2)]
        Op = [psum(f"attn_out{k}") for k in range(2)]
        Dn = [psum(f"dense{k}") for k in range(2)]

        ident = keep("ident", [P, P])
        macc = keep("mask_totals", [P, 16], BF16)
        ones_b = keep("ones_b", [P, P], BF16)
        upper = keep("upper_b", [P, P], BF16)
        desc = keep("desc", [P, E])
        g2c, b2c = keep("g2c", [P, KD]), keep("b2c", [P, KD])

        part_a = ExitStack()

        def sa(name, shape, dt=F32):
            return part_a.enter_context(nc.sbuf_tensor(name, shape, dt))

        def pair(name, shape):
            return sa(name + "_hi", shape, F32R), sa(name + "_lo", shape, F32R)

        Wqs, Wks, Wvs = (pair(n, [P, KD, H * HD]) for n in ("Wq", "Wk", "Wv"))
        Wos = pair("Wo", [P, HT, D])
        swqs, swks = (pair(n, [P, KD, ST * P]) for n in ("swq", "swk"))
        swvs, swos = (pair(n, [P, KD, D]) for n in ("swv", "swo"))
        QT, KT = pair("QT", [P, HT, S]), pair("KT", [P, HT, S])
        Vx = sa("Vx", [P, TT, H, HD + 1])
        U = sa("transposed", [P, 16, S], F32R)
        OT = U[:, 0:8, :], U[:, 8:16, :]
        zT = U[:, 0:2, :], U[:, 2:4, :]
        cT = U[:, 4:6, :], U[:, 6:8, :]
        nT = U[:, 8:10, :], U[:, 10:12, :]
        O2T = U[:, 12:14, :], U[:, 14:16, :]
        O = sa("O", [P, TT, H * HD])
        PT = sa("PT", [P, 4, TT * S])
        QA = sa("self_q", [P, ST, S], F32R)
        KB = pair("self_k", [P, ST, S])
        Vs = sa("Vs", [P, TT, H, SD + 1])
        O2 = sa("O2", [P, TT, D])
        tf = sa("affine_T", [P, KD, S])
        xt, ct, tn, xb, z, zk, xk, n2 = (sa(n, [P, TT, D]) for n in
                                         ("xt", "ct", "tn", "xb", "z", "zk", "xk", "n2"))
        xq, tq = tf, U[:, 12:14, :]
        bv_r, bo_r, sbv_r, sbo_r = sa("bv_r", [P, H * HD]), sa("bo_r", [P, D]), sa("sbv_r", [P, D]), sa("sbo_r", [P, D])
        bqc, bkc = sa("bqc", [P, HT]), sa("bkc", [P, HT])
        sbqc, sbkc = sa("sbqc", [P, ST]), sa("sbkc", [P, ST])
        g1c, b1c = sa("g1c", [P, KD]), sa("b1c", [P, KD])
        wrs = sa("wrs", [P, KD, E])
        nm = sa("neg_max", [P, TT, P])
        mT = sa("neg_max_T", [P, S], F32R)
        pick_x, pick_y = sa("pick_x", [P, HT], F32R), sa("pick_y", [P, ST], F32R)
        lo_row, sign_row = sa("lo_row", [P, 1]), sa("sign_row", [P, 1])
        irow = sa("irow", [P, 1], I32)
        neghalf = sa("neghalf", [P, TT])
        rcx, rcy = sa("rcx", [P, 2, 4]), sa("rcy", [P, 2, H])
        stats = {n: (sa(f"st_{n}", [P, TT, 6]), sa(f"mv_{n}", [P, TT, 2]), sa(f"rs_{n}", [P, TT]))
                 for n in ("x", "z", "n1", "n2")}
        R = sa("route", [P, TT, 16])
        eq = sa("eq", [P, TT, E])
        m1, L2 = sa("m1", [P, TT, E]), sa("L2", [P, TT, E])
        M = sa("masks", [P, TT, 2, E], BF16)
        mr = sa("masked_ranks", [P, TT, 2, E])
        slot = sa("slot", [P, TT, 2])
        oob = sa("oob", [P, TT, 2])
        slot_u = sa("slot_u", [P, TT, 2], U32)
        tok_f = sa("tok_f", [P, TT])
        tok_i = sa("tok_i", [P, TT], I32)
        part_a.close()

        part_c = ExitStack()

        def sc(name, shape, dt=F32):
            return part_c.enter_context(nc.sbuf_tensor(name, shape, dt))

        w1s, w2s = sc("w1s", [P, KD, F]), sc("w2s", [P, FT, D])
        W1 = [(sc(f"W1h{k}", [P, KD, F], F32R), sc(f"W1l{k}", [P, KD, F], F32R)) for k in range(2)]
        W2 = [(sc(f"W2h{k}", [P, FT, D], F32R), sc(f"W2l{k}", [P, FT, D], F32R)) for k in range(2)]
        b1e = [sc(f"b1e{k}", [P, FT]) for k in range(2)]
        b2e = [sc(f"b2e{k}", [P, D]) for k in range(2)]
        Xg = [sc(f"Xg{k}", [P, 2, D]) for k in range(2)]
        XTf = sc("XTf", [P, KD, 256])
        XT = [(sc(f"XTh{k}", [P, KD, 256], F32R), sc(f"XTl{k}", [P, KD, 256], F32R)) for k in range(2)]
        hid = [sc(f"hid{k}", [P, 2, 256]) for k in range(2)]
        HT_ = [(sc(f"Hh{k}", [P, FT, 256], F32R), sc(f"Hl{k}", [P, FT, 256], F32R)) for k in range(2)]
        ys = [sc(f"ys{k}", [P, 2, D]) for k in range(2)]
        gi = [sc(f"gi{k}", [P, 2], U32) for k in range(2)]
        NT = T // P
        Ra = sc("route_all", [P, B, TT, 16])
        NI = E * C // P
        tabs, tabf = sc("tabs", [NI, 2, P], I32), sc("tabf", [NI, 2, P])
        spos_i, spos = sc("spos_i", [NI, P], I32), sc("spos", [NI, P])
        own_e, cnt_own = sc("own_e", [NI, E]), sc("cnt_own", [NI, 1])
        cnt = sc("cnt", [P, 2 * E])
        ids_u = sc("ids_u", [P, NI], U32)
        ex = sc("ex", [P, NT, E])
        bb = [sc(f"bb{k}", [P, NT]) for k in range(9)]
        gidx = [sc(f"gidx{j}", [P, NT], U32) for j in range(2)]
        gate = [sc(f"gate{j}", [P, NT]) for j in range(2)]
        UD = 4
        ya = [[sc(f"ya{j}_{k}", [P, D]) for k in range(UD)] for j in range(2)]
        ba = [sc(f"ba{k}", [P, D]) for k in range(UD)]
        ci = [sc(f"ci{j}", [P, UD], U32) for j in range(2)]
        cg = [sc(f"cg{j}", [P, UD]) for j in range(2)]
        part_c.close()

        ld_w = [sem(f"ld_wt{k}") for k in range(8)]
        ld_small, ld_x, ld_c, ld_r = sem("ld_small"), sem("ld_x"), sem("ld_c"), sem("ld_r")
        w_hi, w_lo = sem("w_hi"), sem("w_lo")
        pool_consts, consts = sem("pool_consts"), sem("consts")
        zeroed = [sem("table0_zeroed"), sem("table1_zeroed")]
        mv_done = {n: sem(f"mv_{n}") for n in ("x", "z", "n1", "n2")}
        rs_done = {n: sem(f"rs_{n}") for n in ("x", "z", "n1", "n2")}
        rs_link = {n: sem(f"rs_link_{n}") for n in ("x", "z", "n1", "n2")}
        bn_link = {n: sem(f"bn_link_{n}") for n in ("x", "z", "n1", "n2")}
        ln_done = {n: sem(f"ln_{n}") for n in ("x", "z", "n1", "n2")}
        N = {"P1": 14, "XO": 6, "P2": 6, "P3a": 2, "P3b": 2}
        full = {n: sem(f"full_{n}") for n in N}
        hi = {n: sem(f"hi_{n}") for n in N}
        free = {n: sem(f"free_{n}") for n in N}
        x1_full, y1_full = sem("x1_full"), sem("y1_full")
        x1_max, y1_max = sem("x1_max"), sem("y1_max")
        negx_full, negy_full = sem("negx_full"), sem("negy_full")
        negx, negy = sem("negx"), sem("negy")
        x2_full, y2_full = sem("x2_full"), sem("y2_full")
        x2_exp, y2_exp = sem("x2_exp"), sem("y2_exp")
        x2_av, y2_av = sem("x2_av"), sem("y2_av")
        rec_x, rec_y = sem("rec_x"), sem("rec_y")
        xo_norm, yo_norm = sem("xo_norm"), sem("yo_norm")
        xb_ready, zk_ready, xk_ready, base_ready = sem("xb_ready"), sem("zk_ready"), sem("xk_ready"), sem("base_ready")
        st_base, st_n2, st_r = sem("st_base"), sem("st_n2"), sem("st_r")
        q_link = sem("q_link")
        tf_ready = sem("tf_ready")
        t2_full, h2_ready = sem("t2_full"), sem("h2_ready")
        route_link, masks_ready, macc_ready = sem("route_link"), sem("masks_ready"), sem("macc_ready")
        slots_ready, route_ready = sem("slots_ready"), sem("route_ready")
        scat = [sem(f"scattered{k}") for k in range(4)]

        def split(src, w):
            return [(src, w[0], w[1])]

        def doubled(src, w):
            v = [m[:, :, :].rearrange("p k (h s r) -> p k h s r", s=2, r=SD) for m in w]
            src = src.rearrange("p k (h r) -> p k h r", r=SD)
            return [(src[:, k], v[0][:, k, :, s, :], v[1][:, k, :, s, :]) for k in range(KD) for s in range(2)]

        def wide(buf):
            return buf.rearrange("p (k n) -> p k n", k=KD)

        vx_flat = Vx[:, :, :, :].rearrange("p t h d -> p (t h d)")[:, 0:KD * H * HD]
        pt_flat = PT[:, :, :].rearrange("p a b -> p (a b)")
        o_flat = O[:, :, :].rearrange("p a b -> p (a b)")

        def by_row(w):
            return w.rearrange("(k p) n -> p k n", p=P)

        weight_parts = [
            ((O[:, :, :], by_row(Wq.rearrange("m h d -> m (h d)"))), split(O[:, :, :], [m[:, :, :] for m in Wqs])),
            ((wide(vx_flat), by_row(Wk.rearrange("m h d -> m (h d)"))), split(wide(vx_flat), [m[:, :, :] for m in Wks])),
            ((wide(pt_flat), by_row(Wv.rearrange("m h d -> m (h d)"))), split(wide(pt_flat), [m[:, :, :] for m in Wvs])),
            ((zk[:, :, :], by_row(swq)), doubled(zk[:, :, :], swqs)),
            ((z[:, :, :], by_row(swk)), doubled(z[:, :, :], swks)),
            ((xk[:, :, :], by_row(swv)), split(xk[:, :, :], [m[:, :, :] for m in swvs])),
            ((n2[:, :, :], by_row(swo)), split(n2[:, :, :], [m[:, :, :] for m in swos])),
            ((o_flat.rearrange("p (t n) -> p t n", n=D), by_row(Wo.rearrange("h d n -> (h d) n"))),
             split(o_flat.rearrange("p (t n) -> p t n", n=D), [m[:, :, :] for m in Wos])),
        ]
        SMALL = 27

        blk = whole.enter_context(nc.Block())

        def first(b, n=1):
            return isinstance(b, int) and b < n

        def hold(eng, s, value):
            eng.wait_ge(s, value)
            if not isinstance(value, int):
                eng.nop(nofuse=True)

        class Chain:

            def __init__(self, eng, s, per, b):
                self.eng, self.s, self.at, self.per, self.n = eng, s, b * per, per, 0

            def __call__(self, ins):
                self.n += 1
                ins.then_inc(self.s, 1)
                self.eng.wait_ge(self.s, self.at + self.n)

            def done(self):
                assert self.n == self.per, self.n

        def iterations(eng, body):
            body(0), body(1)
            with eng.Fori(2, B - 1) as i:
                body(i)
            body(B - 1), body(B), body(B + 1)

        def has(b):
            return not isinstance(b, int) or 0 <= b < B

        ORDER = [("P3b", -2), ("P1", 1), ("XO", 0), ("P2", 0), ("P3a", -1)]

        def wait_dense(eng, stage, b):
            k = [s for s, _ in ORDER].index(stage)
            i = b - ORDER[k][1]
            while True:
                k -= 1
                if k < 0:
                    k, i = len(ORDER) - 1, i - 1
                s, off = ORDER[k]
                if isinstance(i, int) and i < -1:
                    return
                if has(i + off) and not (isinstance(i, int) and i == -1 and s != "P1"):
                    eng.wait_ge(free[s], (i + off) * N[s] + N[s])
                    return

        def bank(ps, n=2):
            return ps[:, :].rearrange("p (a c) -> p a c", a=n)

        def three(pe, outp, lhs, rhs, a, b, start, stop):
            pe.matmul(outp, a(lhs[0]), b(rhs[0]), start=start, stop=False)
            pe.matmul(outp, a(lhs[1]), b(rhs[0]), start=False, stop=False)
            return pe.matmul(outp, a(lhs[0]), b(rhs[1]), start=False, stop=stop)

        def pe_transpose_in(pe, src, dst):
            for t in range(TT):
                for k in range(KD):
                    last = pe.transpose(bank(dst)[:, k, t * P:(t + 1) * P], src[:, t, k * P:(k + 1) * P], ident[:, :])
            return last

        def pe_project(pe, stage, b, job, w, act_t, t0):
            for j in range(2):
                for k in range(KD):
                    last = three(pe, bank(Dn[job % 2])[:, j, :], w, act_t,
                                 lambda m, k=k, j=j: m[:, k, (t0 + j) * P:(t0 + j + 1) * P],
                                 lambda m, k=k: m[:, k, :], k == 0, k == KD - 1)
            last.then_inc(full[stage], 1)

        def pe_P1(pe, b):
            wait_dense(pe, "P1", b)
            pe.wait_ge(ln_done["x"], b + 1)
            pe_transpose_in(pe, tn, Dn[0]).then_inc(full["P1"], 1)
            pe.wait_ge(ld_c, (b + 1) * 16)
            pe_transpose_in(pe, ct, Dn[1]).then_inc(full["P1"], 1)
            for job in range(2, 14):
                pe.wait_ge(free["P1"], b * 14 + job - 1)
                if job < 6:
                    pe_project(pe, "P1", b, job, Wqs, zT, 2 * (job - 2))
                elif job < 10:
                    pe_project(pe, "P1", b, job, Wks, cT, 2 * (job - 6))
                else:
                    t, half = divmod(job - 10, 2)
                    for k in range(KD):
                        last = three(pe, Dn[job % 2][:, :], cT, Wvs, lambda m: m[:, k, t * P:(t + 1) * P],
                                     lambda m: m[:, k, half * 512:(half + 1) * 512], k == 0, k == KD - 1)
                    last.then_inc(full["P1"], 1)

        def pe_X1(pe, b, h):
            rows, t = slice(64 * (h % 2), 64 * (h % 2) + 64), h // 2
            if h == 0:
                pe.wait_ge(free["P1"], b * 14 + 10)
            if h >= 2:
                pe.wait_ge(x1_max, b * H + h - 1)
            elif not first(b, 2):
                pe.wait_ge(negy, b - 1)
            elif b == 1 and h == 0:
                pe.wait_ge(negx, 1)
            for q in range(TT):
                last = pe.matmul(bank(Sn[h % 2])[:, q, :], QT[0][rows, t, q * P:(q + 1) * P], KT[0][rows, t, :],
                                 start=True, stop=True)
            last.then_inc(x1_full, 1)

        def pe_Y1(pe, b, h):
            rows, t = slice(32 * (h % 4), 32 * (h % 4) + 32), h // 4
            if h == 0:
                pe.wait_ge(free["P2"], b * 6 + 6)
            if h >= 2:
                pe.wait_ge(y1_max, b * H + h - 1)
            elif h == 0:
                pe.wait_ge(negx, b + 2 if has(b + 1) else b + 1)
            for q in range(TT):
                last = pe.matmul(bank(Sn[h % 2])[:, q, :], QA[rows, t, q * P:(q + 1) * P], KB[0][rows, t, :],
                                 start=True, stop=True)
            last.then_inc(y1_full, 1)

        def pe_neg(pe, b, maxes, done, nm, s):
            pe.wait_ge(done, b * H + H)
            for q in range(TT):
                last = pe.transpose(Sn[0][:, q * P:(q + 1) * P], nm[:, q, :], ident[:, :])
            last.then_inc(s, 1)

        def scores_free(pe, b, h, mine, cross):
            if h >= 2:
                pe.wait_ge(mine, b * H + h - 1)
            elif cross:
                if not first(b, 2):
                    pe.wait_ge(y2_exp, (b - 1) * H)
                elif b == 1:
                    pe.wait_ge(x2_exp, H)
            else:
                if has(b + 1):
                    pe.wait_ge(x2_exp, (b + 2) * H)
                else:
                    pe.wait_ge(y2_exp, b * H)

        def pe_X2(pe, b, h):
            rows, t = slice(64 * (h % 2), 64 * (h % 2) + 64), h // 2
            if h == 0:
                pe.wait_ge(negx, b + 1)
            scores_free(pe, b, h, x2_exp, True)
            for k in range(TT):
                o = bank(Sp[h % 2])[:, k, :]
                three(pe, o, KT, QT, lambda m: m[rows, t, k * P:(k + 1) * P], lambda m: m[rows, t, :], True, False)
                last = pe.matmul(o, pick_x[rows, t:t + 1].to_broadcast([64, P]), mT[rows, :], start=False, stop=True)
            last.then_inc(x2_full, 1)

        def pe_Y2(pe, b, h):
            rows, t = slice(32 * (h % 4), 32 * (h % 4) + 32), h // 4
            if h == 0:
                pe.wait_ge(negy, b + 1)
            scores_free(pe, b, h, y2_exp, False)
            for k in range(TT):
                o = bank(Sp[h % 2])[:, k, :]
                for n, kb in enumerate(KB):
                    pe.matmul(o, kb[rows, t, k * P:(k + 1) * P], QA[rows, t, :], start=n == 0, stop=False)
                last = pe.matmul(o, pick_y[rows, t:t + 1].to_broadcast([32, P]), mT[rows, :], start=False, stop=True)
            last.then_inc(y2_full, 1)

        def pe_XAV(pe, b, h):
            g, hh = divmod(h, 2)
            if h == 0:
                pe.wait_ge(free["P1"], b * 14 + 14)
                if first(b):
                    pe.wait_ge(vx_ones, 1)
            if hh == 0:
                if g >= 2:
                    pe.wait_ge(xo_norm, b * GX + g - 1)
                elif not first(b, 2):
                    pe.wait_ge(yo_norm, (b - 1) * GY)
                elif b == 1:
                    pe.wait_ge(xo_norm, GX)
            pe.wait_ge(x2_exp, b * H + h + 1)
            o = Op[g % 2][:, 0:TT * 2 * (HD + 1)].rearrange("p (q a c) -> p q a c", q=TT, a=2)
            for q in range(TT):
                for k in range(TT):
                    last = pe.matmul(o[:, q, hh, :], PT[:, h % 4, k * S + q * P:k * S + (q + 1) * P], Vx[:, k, h, :],
                                     start=k == 0, stop=k == TT - 1)
            last.then_inc(x2_av, 1)

        def pe_YAV(pe, b, h):
            g, hh = divmod(h, H // GY)
            if hh == 0:
                if has(b + 1):
                    pe.wait_ge(xo_norm, (b + 2) * GX)
                else:
                    pe.wait_ge(yo_norm, b * GY)
            pe.wait_ge(y2_exp, b * H + h + 1)
            o = Op[g % 2][:, 0:TT * 8 * (SD + 1)].rearrange("p (q a c) -> p q a c", q=TT, a=8)
            for q in range(TT):
                for k in range(TT):
                    last = pe.matmul(o[:, q, hh, :], PT[:, h % 4, k * S + q * P:k * S + (q + 1) * P], Vs[:, k, h, :],
                                     start=k == 0, stop=k == TT - 1)
            last.then_inc(y2_av, 1)

        def pe_XO(pe, b):
            wait_dense(pe, "XO", b)
            for job in range(4):
                if job >= 2:
                    pe.wait_ge(free["XO"], b * 6 + job - 1)
                pe.wait_ge(xo_norm, b * GX + 2 * job + 2)
                for j in range(2):
                    for q in range(TT):
                        t = 2 * job + j
                        last = pe.transpose(bank(Dn[job % 2])[:, j, q * P:(q + 1) * P], O[:, q, t * P:(t + 1) * P],
                                            ident[:, :])
                last.then_inc(full["XO"], 1)
            pe.wait_ge(free["XO"], b * 6 + 4)
            for q in range(TT):
                for t in range(HT):
                    last = three(pe, Dn[q][:, 0:D], OT, Wos, lambda m: m[:, t, q * P:(q + 1) * P],
                                 lambda m: m[:, t, :], t == 0, t == HT - 1)
                last.then_inc(full["XO"], 1)

        def pe_P2(pe, b):
            wait_dense(pe, "P2", b)
            pe.wait_ge(ln_done["n1"], b + 1)
            pe_transpose_in(pe, tn, Dn[0]).then_inc(full["P2"], 1)
            pe.wait_ge(free["P2"], b * 6 + 1)
            for job in range(1, 6):
                if job >= 2:
                    pe.wait_ge(free["P2"], b * 6 + job - 1)
                if job < 3:
                    pe_project(pe, "P2", b, job, swqs, nT, 2 * (job - 1))
                elif job < 5:
                    pe_project(pe, "P2", b, job, swks, nT, 2 * (job - 3))
                else:
                    for t in range(TT):
                        for k in range(KD):
                            last = three(pe, bank(Dn[1])[:, t, :], nT, swvs, lambda m: m[:, k, t * P:(t + 1) * P],
                                         lambda m: m[:, k, :], k == 0, k == KD - 1)
                    last.then_inc(full["P2"], 1)

        def pe_P3a(pe, b):
            wait_dense(pe, "P3a", b)
            pe.wait_ge(yo_norm, b * GY + GY)
            pe_transpose_in(pe, O2, Dn[0]).then_inc(full["P3a"], 1)
            pe.wait_ge(free["P3a"], b * 2 + 1)
            for q in range(TT):
                for t in range(KD):
                    last = three(pe, bank(Dn[1])[:, q, :], O2T, swos, lambda m: m[:, t, q * P:(q + 1) * P],
                                 lambda m: m[:, t, :], t == 0, t == KD - 1)
            last.then_inc(full["P3a"], 1)

        def pe_P3b(pe, b, part):
            if part == 0:
                wait_dense(pe, "P3b", b)
                pe.wait_ge(ln_done["n2"], b + 1)
                pe_transpose_in(pe, n2, Dn[0]).then_inc(t2_full, 1)
            elif part == 1:
                pe.wait_ge(h2_ready, b + 1)
                for t in range(TT):
                    for k in range(KD):
                        last = pe.matmul(Dn[1][:, t * E:(t + 1) * E], tf[:, k, t * P:(t + 1) * P], wrs[:, k, :],
                                         start=k == 0, stop=k == KD - 1)
                last.then_inc(full["P3b"], 1)
            else:
                pe.wait_ge(masks_ready, b + 1)
                pe.wait_ge(macc_ready, b + 1)
                mm = [M[:, t, :, :].rearrange("p a e -> p (a e)") for t in range(TT)]
                pe.matmul(Dn[0][:, 0:16], upper[:, :], mm[0], start=True, stop=False)
                pe.matmul(Dn[0][:, 0:16], ones_b[:, :], macc[:, :], start=False, stop=True)
                pe.matmul(Dn[0][:, 16:32], upper[:, :], mm[1], start=True, stop=False)
                pe.matmul(Dn[0][:, 16:32], ones_b[:, :], mm[0], start=False, stop=False)
                last = pe.matmul(Dn[0][:, 16:32], ones_b[:, :], macc[:, :], start=False, stop=True)
                last.then_inc(full["P3b"], 1)

        cnt_full, idsT_full = sem("cnt_full"), sem("idsT_full")
        xt_hi, cg_ready, pick_link, pool_link, vx_ones, pool_b2, ld_tab2 = (sem(n) for n in (
            "xt_hi", "cg_ready", "pick_link", "pool_link", "vx_ones", "pool_b2", "ld_tab2"))
        ld_b1, ld_b2 = [sem(f"ld_b1_{k}") for k in range(2)], [sem(f"ld_b2_{k}") for k in range(2)]
        cx_full, m1_full, m2_full = sem("cx_full"), sem("m1_full"), sem("m2_full")
        xt_ready, relu_done, h_hi, h_ready, y_ready = (sem(n) for n in ("xt_ready", "relu_done", "h_hi", "h_ready", "y_ready"))
        xtf_ready = sem("xtf_ready")
        gath = [[sem(f"gathered{k}_{q}") for q in range(2)] for k in range(2)]
        gi_ready = sem("gi_ready")
        ld_w1, ld_w2 = sem("ld_w1"), sem("ld_w2")
        we_hi, we_lo = sem("we_hi"), sem("we_lo")
        st_y = [sem(f"st_y{k}") for k in range(2)]
        b_link, ids_sel, ids_ready, pool_b = sem("b_link"), sem("ids_sel"), sem("ids_ready"), sem("pool_b")
        ld_route, ld_tab = sem("ld_route"), sem("ld_tab")
        exb_in, exb = sem("exb_in"), sem("exb")
        gates_ready = sem("gates_ready")
        phase_a_done = sem("phase_a_done")
        ciq = sem("ciq")
        ciu = sem("ciu")
        gd = [[sem(f"gd{j}_{k}") for k in range(UD)] for j in range(2)]
        ldb = [sem(f"ldb{k}") for k in range(UD)]
        sto = [sem(f"sto{k}") for k in range(UD)]
        comb_mid, comb = sem("comb_mid"), sem("comb")

        NG = E * C // 256
        TB, MB, YB = Sp[0], [Sp[1], Sn[0], Sn[1], Op[0]], [Op[1], Dn[0]]

        def groups(eng, body):
            body(0)
            with eng.Fori(1, NG // 8 - 1) as j:
                body(j)
            body(NG // 8 - 1)

        def c_T(pe, j, k):
            g, r = j * 8 + k, k % 2
            n = j * 4 + k // 2
            for q in range(2):
                pe.wait_ge(gath[r][q], n * 16 + 16)
            if not (first(j) and k == 0):
                pe.wait_ge(xtf_ready, g)
            for q in range(2):
                for d in range(KD):
                    last = pe.transpose(bank(TB)[:, d, q * P:(q + 1) * P], Xg[r][:, q, d * P:(d + 1) * P], ident[:, :])
            last.then_inc(cx_full, 1)

        def c_M1(pe, j, k):
            g, e2 = j * 8 + k, k // 4
            if k % 4 == 0:
                pe.wait_ge(we_lo, (j * 2 + e2 + 1) * 2)
            pe.wait_ge(xt_ready, g + 1)
            for c in range(4):
                if not (first(j) and k == 0):
                    pe.wait_ge(relu_done, g * 4 + c - 3)
                for i2 in range(2):
                    f = 2 * c + i2
                    for d in range(KD):
                        last = three(pe, bank(MB[c])[:, i2, :], W1[e2], XT[k % 2], lambda m: m[:, d, f * P:(f + 1) * P],
                                     lambda m: m[:, d, :], d == 0, d == KD - 1)
                last.then_inc(m1_full, 1)

        def c_M2(pe, j, k):
            g, e2, r = j * 8 + k, (k // 4) % 2, k % 2
            pe.wait_ge(h_ready, g * 4 + 4)
            if not (first(j) and k < 2):
                pe.wait_ge(y_ready, g - 1)
            for q in range(2):
                for f in range(FT):
                    last = three(pe, bank(YB[r])[:, q, :], HT_[r], W2[e2], lambda m: m[:, f, q * P:(q + 1) * P],
                                 lambda m: m[:, f, :], f == 0, f == FT - 1)
            last.then_inc(m2_full, 1)

        @blk.tensor
        def _(pe):
            pe.wait_ge(consts, 4)
            pe.wait_ge(pick_link, 2)
            pe.wait_ge(w_lo, 8)
            pe_P1(pe, 0)
            for h in range(H):
                pe_X1(pe, 0, h)
            pe_neg(pe, 0, None, x1_max, nm, negx_full)

            def body(i):
                X, Y, Z, W = has(i), has(i - 1), has(i + 1), has(i - 2)
                for h in range(H + 1):
                    if X and h < H:
                        pe_X2(pe, i, h)
                    if Y and h < H:
                        pe_Y1(pe, i - 1, h)
                    if X and h:
                        pe_XAV(pe, i, h - 1)
                    if W and h in (4, 8, 12):
                        pe_P3b(pe, i - 2, h // 4 - 1)
                if Z:
                    pe_P1(pe, i + 1)
                if Y:
                    pe_neg(pe, i - 1, None, y1_max, nm, negy_full)
                if X:
                    pe_XO(pe, i)
                for h in range(H + 1):
                    if Y and h < H:
                        pe_Y2(pe, i - 1, h)
                    if Z and h < H:
                        pe_X1(pe, i + 1, h)
                    if Y and h:
                        pe_YAV(pe, i - 1, h - 1)
                if X:
                    pe_P2(pe, i)
                if Z:
                    pe_neg(pe, i + 1, None, x1_max, nm, negx_full)
                if Y:
                    pe_P3a(pe, i - 1)

            iterations(pe, body)
            pe.wait_ge(macc_ready, B + 1)
            pe.matmul(Dn[1][:, 0:16], ones_b[:, :], macc[:, :], start=True, stop=True).then_inc(cnt_full, 1)
            pe.wait_ge(ids_sel, 1)
            pe.transpose(Dn[0][:, 0:NI], tabf[:, 0, :], ident[0:NI, 0:NI]).then_inc(idsT_full, 1)
            c_T(pe, 0, 0)

            def body_c(j):
                for k in range(8):
                    if k < 7 or not (isinstance(j, int) and j == NG // 8 - 1):
                        c_T(pe, j, k + 1) if k < 7 else c_T(pe, j + 1, 0)
                    c_M1(pe, j, k)
                    if k or not first(j):
                        c_M2(pe, j, k - 1)

            groups(pe, body_c)
            c_M2(pe, NG // 8 - 1, 7)

        @blk.scalar
        def _(act):
            for n, (ld, parts) in enumerate(weight_parts):
                act.wait_ge(ld_w[n], 16)
                for src, h, _ in parts:
                    last = act.activation(h, src, ACT.Copy)
                last.then_inc(w_hi, 1)

            def P1(b):
                for job in range(10):
                    act.wait_ge(full["P1"], b * 14 + job + 1)
                    if job < 2:
                        act.activation((zT, cT)[job][0], bank(Dn[job % 2]), ACT.Copy).then_inc(hi["P1"], 1)
                    else:
                        dst, bias = (QT, bqc) if job < 6 else (KT, bkc)
                        t0 = 2 * ((job - 2) % 4)
                        for j in range(2):
                            last = act.activation(dst[0][:, t0 + j, :], bank(Dn[job % 2])[:, j, :], ACT.Identity,
                                                  bias=bias[:, t0 + j:t0 + j + 1])
                        last.then_inc(hi["P1"], 1)

            def neg(b, f, dst, s):
                act.wait_ge(f, b + 1)
                act.activation(dst[:, :], Sn[0][:, 0:S], ACT.Copy).then_inc(s, 1)

            def expo(b, h, f, s, scale, av, prev):
                act.wait_ge(f, b * H + h + 1)
                if h >= 4:
                    act.wait_ge(av, b * H + h - 3)
                elif h == 0 and prev is not None:
                    act.wait_ge(*prev)
                act.activation(PT[:, h % 4, :], Sp[h % 2][:, :], ACT.Exp, scale=scale).then_inc(s, 1)

            def P3b(b):
                act.wait_ge(t2_full, b + 1)
                for k in range(KD):
                    last = act.activation(tf[:, k, :], bank(Dn[0])[:, k, :], ACT.Identity, scale=g2c[:, k:k + 1],
                                          bias=b2c[:, k:k + 1])
                last.then_inc(h2_ready, 1)

            def XO(b):
                for job in range(4):
                    act.wait_ge(full["XO"], b * 6 + job + 1)
                    act.activation(OT[0][:, 2 * job:2 * job + 2, :], bank(Dn[job % 2]), ACT.Copy).then_inc(hi["XO"], 1)

            def P2(b):
                act.wait_ge(full["P2"], b * 6 + 1)
                for k in range(KD):
                    last = act.activation(tf[:, k, :], bank(Dn[0])[:, k, :], ACT.Identity, scale=g1c[:, k:k + 1],
                                          bias=b1c[:, k:k + 1])
                last.then_inc(tf_ready, 1)
                act.wait_ge(tf_ready, b + 1)
                act.activation(nT[0], tf[:, :, :], ACT.Copy).then_inc(hi["P2"], 1)
                for job in range(1, 3):
                    act.wait_ge(q_link, b * 2 + job)
                    act.activation(tq, xq[:, :, :], ACT.Copy, scale=sign_row[:, 0:1]).then_inc(hi["P2"], 1)
                for job in range(3, 5):
                    act.wait_ge(full["P2"], b * 6 + job + 1)
                    t0 = 2 * (job - 3)
                    for j in range(2):
                        last = act.activation(KB[0][:, t0 + j, :], bank(Dn[job % 2])[:, j, :], ACT.Identity,
                                              bias=sbkc[:, t0 + j:t0 + j + 1])
                    last.then_inc(hi["P2"], 1)

            def P3a(b):
                act.wait_ge(full["P3a"], b * 2 + 1)
                act.activation(O2T[0], bank(Dn[0]), ACT.Copy).then_inc(hi["P3a"], 1)

            act.wait_ge(consts, 4)
            act.wait_ge(ld_small, 16 * SMALL)
            act.wait_ge(w_lo, 8)
            P1(0)
            neg(0, negx_full, mT, negx)

            def body(i):
                X, Y, Z, W = has(i), has(i - 1), has(i + 1), has(i - 2)
                for h in range(H):
                    if X:
                        prev = None if first(i) else (x2_av, H) if first(i, 2) else (y2_av, (i - 1) * H)
                        expo(i, h, x2_full, x2_exp, XS, x2_av, prev)
                    if W and h == 5:
                        P3b(i - 2)
                if Z:
                    P1(i + 1)
                if Y:
                    neg(i - 1, negy_full, mT, negy)
                if X:
                    XO(i)
                for h in range(H):
                    if Y:
                        expo(i - 1, h, y2_full, y2_exp, YS, y2_av, (x2_av, (i + 1) * H) if X else (y2_av, (i - 1) * H))
                if X:
                    P2(i)
                if Z:
                    neg(i + 1, negx_full, mT, negx)
                if Y:
                    P3a(i - 1)

            iterations(act, body)

            def weights(e, e2):
                act.wait_ge(ld_w1, e * 16 + 16)
                if not first(e, 2):
                    act.wait_ge(m1_full, (e - 1) * 16)
                act.activation(W1[e2][0][:, :, :], w1s[:, :, :], ACT.Copy).then_inc(we_hi, 1)
                act.wait_ge(ld_w2, e * 16 + 16)
                if not first(e, 2):
                    act.wait_ge(m2_full, (e - 1) * 4)
                act.activation(W2[e2][0][:, :, :], w2s[:, :, :], ACT.Copy).then_inc(we_hi, 1)

            def xtf(j, k):
                g = j * 8 + k
                act.wait_ge(cx_full, g + 1)
                if not (first(j) and k == 0):
                    act.wait_ge(xt_ready, g)
                for d in range(KD):
                    last = act.activation(XTf[:, d, :], bank(TB)[:, d, :], ACT.Identity, scale=g2c[:, d:d + 1],
                                          bias=b2c[:, d:d + 1])
                last.then_inc(xtf_ready, 1)

            def relu(j, k):
                g = j * 8 + k
                if k % 4 == 0:
                    act.wait_ge(ld_b1[k // 4], j * 16 + 16)
                for c in range(4):
                    act.wait_ge(m1_full, g * 4 + c + 1)
                    if not (first(j) and k == 0 and c < 2):
                        act.wait_ge(h_ready, g * 4 + c - 1)
                    for i2 in range(2):
                        last = act.activation(hid[c % 2][:, i2, :], bank(MB[c])[:, i2, :], ACT.Relu,
                                              bias=b1e[k // 4][:, 2 * c + i2:2 * c + i2 + 1])
                    last.then_inc(relu_done, 1)

            act.wait_ge(ids_ready, 1)
            weights(0, 0)
            xtf(0, 0)
            act.wait_ge(exb_in, 1)
            act.activation(ex[:, :, :], ex[:, :, :], ACT.Exp).then_inc(exb, 1)
            act.wait_ge(exb_in, 2)
            act.activation(bb[2][:, :], bb[2][:, :], ACT.Exp).then_inc(exb, 1)

            def body_c(j):
                for k in range(8):
                    if k % 4 == 1 and not (k == 5 and isinstance(j, int) and j == NG // 8 - 1):
                        weights(j * 2 + k // 4 + 1, 1 - k // 4)
                    if k < 7 or not (isinstance(j, int) and j == NG // 8 - 1):
                        xtf(j, k + 1) if k < 7 else xtf(j + 1, 0)
                    relu(j, k)

            groups(act, body_c)


        @blk.vector
        def _(dve):
            def f32(ap):
                return ap.bitcast(F32)

            dve.wait_ge(pool_consts, 1)
            dve.tensor_tensor(pick_x[:, :], ident[:, 0:HT], ident[:, 64:64 + HT], ALU.add).then_inc(consts, 1)
            dve.tensor_reduce(eq[:, 0, 0:ST], ident[:, :].rearrange("p (j t) -> p t j", j=4)[:, 0:ST, :], AX_X,
                              ALU.add).then_inc(pick_link, 1)
            dve.wait_ge(pick_link, 1)
            dve.tensor_copy(pick_y[:, :], eq[:, 0, 0:ST]).then_inc(pick_link, 1)
            dve.tensor_scalar(irow[:, :], irow[:, :], 16, None, ALU.bitwise_and).then_inc(consts, 1)
            dve.wait_ge(consts, 2)
            dve.tensor_scalar(lo_row[:, :], irow[:, :], 1.0 / 16, None, ALU.mult).then_inc(consts, 1)
            dve.wait_ge(consts, 3)
            dve.tensor_scalar(sign_row[:, :], lo_row[:, :], 2.0, -1.0, ALU.mult, ALU.add).then_inc(consts, 1)
            for n, (_, parts) in enumerate(weight_parts):
                dve.wait_ge(w_hi, n + 1)
                for src, h, low in parts:
                    last = dve.tensor_tensor(low, src, f32(h), ALU.subtract)
                last.then_inc(w_lo, 1)
            dve.wait_ge(ld_small, 16 * SMALL)

            def ln_stats(n, src, b):
                st, mv, _ = stats[n]
                for t in range(TT):
                    last = dve.bn_stats(st[:, t, :], src[:, t, :])
                last.then_inc(bn_link[n], 1)
                hold(dve, bn_link[n], b + 1)
                for t in range(TT):
                    last = dve.bn_aggr(mv[:, t, :], st[:, t, :])
                last.then_inc(mv_done[n], 1)

            def ln_apply(n, src, dst, b):
                _, mv, rs = stats[n]
                dve.wait_ge(rs_done[n], b + 1)
                for t in range(TT):
                    last = dve.tensor_scalar(dst[:, t, :], src[:, t, :], mv[:, t, 0:1], rs[:, t:t + 1],
                                             ALU.subtract, ALU.mult)
                last.then_inc(ln_done[n], 1)

            def lnx_stats(b):
                dve.wait_ge(ld_x, b * 16 + 16)
                ln_stats("x", xt, b)

            def P1(b):
                for job in range(14):
                    d = Dn[job % 2]
                    if job < 10:
                        dve.wait_ge(hi["P1"], b * 10 + job + 1)
                    else:
                        dve.wait_ge(full["P1"], b * 14 + job + 1)
                    if job < 2:
                        m = (zT, cT)[job]
                        last = dve.tensor_tensor(m[1], bank(d), f32(m[0]), ALU.subtract)
                    elif job < 10:
                        dst, bias = (QT, bqc) if job < 6 else (KT, bkc)
                        t0 = 2 * ((job - 2) % 4)
                        for j in range(2):
                            last = dve.scalar_tensor_tensor(dst[1][:, t0 + j, :], bank(d)[:, j, :],
                                                            bias[:, t0 + j:t0 + j + 1], f32(dst[0][:, t0 + j, :]),
                                                            ALU.add, ALU.subtract)
                    else:
                        t, half = divmod(job - 10, 2)
                        h8 = slice(half * 8, half * 8 + 8)
                        last = dve.tensor_tensor(
                            Vx[:, t, h8, 0:HD], d[:, :].rearrange("p (h c) -> p h c", c=HD),
                            bv_r[:, half * 512:(half + 1) * 512].rearrange("p (h c) -> p h c", c=HD), ALU.add)
                    last.then_inc(free["P1"], 1)

            def row_max(b, h, f, nm, s, tiles):
                dve.wait_ge(f, b * H + h + 1)
                dve.tensor_reduce(nm[:, :, P // tiles * (h % tiles) + h // tiles], bank(Sn[h % 2]), AX_X, ALU.max, negate=True).then_inc(s, 1)

            def normalise(b, g, av, heads, groups, rc, width, dst, link, s):
                dve.wait_ge(av, b * H + heads * (g + 1))
                o = Op[g % 2][:, 0:TT * heads * (width + 1)].rearrange("p (q a c) -> p q a c", q=TT, a=heads)
                r = rc[:, g % 2, :].rearrange("p (q a) -> p q a", q=TT)
                if g >= 2 or not first(b):
                    dve.wait_ge(s, b * groups + g - 1)
                dve.reciprocal(r, o[:, :, :, width]).then_inc(link, 1)
                dve.wait_ge(link, b * groups + g + 1)
                dve.tensor_tensor(dst[:, :, g * heads * width:(g + 1) * heads * width]
                                  .rearrange("p q (a c) -> p q a c", a=heads), o[:, :, :, 0:width],
                                  r.unsqueeze(3).to_broadcast([P, TT, heads, width]), ALU.mult).then_inc(s, 1)

            def xnorm(b, g):
                normalise(b, g, x2_av, 2, GX, rcx, HD, O, rec_x, xo_norm)

            def ynorm(b, g):
                normalise(b, g, y2_av, H // GY, GY, rcy, SD, O2, rec_y, yo_norm)

            def XO(b):
                for job in range(4):
                    dve.wait_ge(hi["XO"], b * 4 + job + 1)
                    o = slice(2 * job, 2 * job + 2)
                    dve.tensor_tensor(OT[1][:, o, :], bank(Dn[job % 2]), f32(OT[0][:, o, :]),
                                      ALU.subtract).then_inc(free["XO"], 1)
                dve.wait_ge(xb_ready, b + 1)
                for q in range(TT):
                    dve.wait_ge(full["XO"], b * 6 + 5 + q)
                    dve.tensor_tensor(xb[:, q, :], Dn[q][:, 0:D], xb[:, q, :], ALU.add).then_inc(free["XO"], 1)

            def P2(b):
                dve.wait_ge(hi["P2"], b * 5 + 1)
                dve.tensor_tensor(nT[1], tf[:, :, :], f32(nT[0]), ALU.subtract).then_inc(free["P2"], 1)
                for job in range(1, 3):
                    t0 = 2 * (job - 1)
                    dve.wait_ge(full["P2"], b * 6 + job + 1)
                    dve.wait_ge(free["P2"], b * 6 + job)
                    for j in range(2):
                        last = dve.tensor_scalar(xq[:, j, :], bank(Dn[job % 2])[:, j, :], sbqc[:, t0 + j:t0 + j + 1],
                                                 None, ALU.add)
                    last.then_inc(q_link, 1)
                    dve.wait_ge(hi["P2"], b * 5 + job + 1)
                    dve.scalar_tensor_tensor(QA[:, t0:t0 + 2, :], xq[:, :, :], lo_row[:, 0:1], f32(tq),
                                             ALU.mult, ALU.subtract).then_inc(free["P2"], 1)
                for job in range(3, 5):
                    t0 = 2 * (job - 3)
                    dve.wait_ge(hi["P2"], b * 5 + job + 1)
                    for j in range(2):
                        last = dve.scalar_tensor_tensor(KB[1][:, t0 + j, :], bank(Dn[job % 2])[:, j, :],
                                                        sbkc[:, t0 + j:t0 + j + 1], f32(KB[0][:, t0 + j, :]),
                                                        ALU.add, ALU.subtract)
                    last.then_inc(free["P2"], 1)
                dve.wait_ge(full["P2"], b * 6 + 6)
                dve.tensor_tensor(Vs[:, :, :, 0:SD], Dn[1][:, :].rearrange("p (t h r) -> p t h r", t=TT, r=SD),
                                  sbv_r[:, :].rearrange("p (h r) -> p h r", r=SD).unsqueeze(1)
                                  .to_broadcast([P, TT, H, SD]), ALU.add).then_inc(free["P2"], 1)

            def P3a(b):
                dve.wait_ge(hi["P3a"], b + 1)
                dve.tensor_tensor(O2T[1], bank(Dn[0]), f32(O2T[0]), ALU.subtract).then_inc(free["P3a"], 1)
                dve.wait_ge(full["P3a"], b * 2 + 2)
                dve.wait_ge(zk_ready, b + 1)
                dve.tensor_tensor(zk[:, :, :], bank(Dn[1]), zk[:, :, :], ALU.add).then_inc(free["P3a"], 1)

            def each(ap, n=TT):
                return ap.unsqueeze(1).to_broadcast([P, n, E])

            def over(ap, n=TT):
                return ap.unsqueeze(2).to_broadcast([P, n, E])

            def router(b):
                dve.wait_ge(full["P3b"], b * 2 + 1)
                if not first(b):
                    dve.wait_ge(st_r, b * 16)
                dve.tensor_copy(R[:, :, 0:E], Dn[1][:, 0:TT * E].rearrange("p (t e) -> p t e", e=E))\
                   .then_inc(free["P3b"], 1)
                dve.wait_ge(free["P3b"], b * 2 + 1)
                link = Chain(dve, route_link, 20, b)
                L = R[:, :, 0:E]
                link(dve.tensor_reduce(R[:, :, 12], L, AX_X, ALU.max))
                link(dve.tensor_tensor(eq[:, :, :], L, over(R[:, :, 12]), ALU.is_equal))
                link(dve.tensor_tensor(m1[:, :, :], eq[:, :, :], each(desc[:, :]), ALU.mult))
                link(dve.tensor_reduce(R[:, :, 10], m1[:, :, :], AX_X, ALU.max))
                link(dve.tensor_tensor(m1[:, :, :], each(desc[:, :]), over(R[:, :, 10]), ALU.is_equal))
                link(dve.scalar_tensor_tensor(L2[:, :, :], m1[:, :, :], -3.0e38, L, ALU.mult, ALU.add))
                link(dve.tensor_reduce(R[:, :, 13], L2[:, :, :], AX_X, ALU.max))
                link(dve.tensor_tensor(eq[:, :, :], L2[:, :, :], over(R[:, :, 13]), ALU.is_equal))
                link(dve.tensor_tensor(L2[:, :, :], eq[:, :, :], each(desc[:, :]), ALU.mult))
                link(dve.tensor_reduce(R[:, :, 11], L2[:, :, :], AX_X, ALU.max))
                link(dve.tensor_copy(M[:, :, 0, :], m1[:, :, :]))
                dve.tensor_tensor(M[:, :, 1, :], each(desc[:, :]), over(R[:, :, 11]), ALU.is_equal)\
                   .then_inc(masks_ready, 1)
                return link

            def ranks(b):
                link = Chain(dve, route_link, 20, b)
                link.n = 11
                dve.wait_ge(full["P3b"], b * 2 + 2)
                dve.wait_ge(masks_ready, b + 1)
                dve.tensor_tensor(mr[:, :, :, :], Dn[0][:, 0:32].rearrange("p (t a e) -> p t a e", t=TT, a=2),
                                  M[:, :, :, :], ALU.mult).then_inc(free["P3b"], 1)
                link(dve.tensor_tensor(macc[:, :], macc[:, :], M[:, 0, :, :].rearrange("p a e -> p (a e)"), ALU.add))
                dve.tensor_tensor(macc[:, :], macc[:, :], M[:, 1, :, :].rearrange("p a e -> p (a e)"), ALU.add)\
                   .then_inc(macc_ready, 1)
                dve.wait_ge(free["P3b"], b * 2 + 2)
                link(dve.tensor_reduce(R[:, :, 8:10], mr[:, :, :, :], AX_X, ALU.add))
                link(dve.tensor_scalar(slot[:, :, :], R[:, :, 10:12], -float(C), float(E * C), ALU.mult, ALU.add))
                link(dve.tensor_tensor(slot[:, :, 0], slot[:, :, 0], R[:, :, 8], ALU.add))
                link(dve.scalar_tensor_tensor(slot[:, :, 1], slot[:, :, 1], float(C - 1), R[:, :, 9],
                                              ALU.add, ALU.subtract))
                link(dve.tensor_scalar(oob[:, :, :], R[:, :, 8:10], float(C), FAR, ALU.is_ge, ALU.mult))
                link(dve.tensor_tensor(slot[:, :, :], slot[:, :, :], oob[:, :, :], ALU.add))
                if not first(b):
                    for s in scat:
                        dve.wait_ge(s, b * 16)
                link(dve.tensor_copy(tok_i[:, :], tok_f[:, :]))
                link(dve.tensor_scalar(tok_f[:, :], tok_f[:, :], float(S), None, ALU.add))
                dve.tensor_copy(slot_u[:, :, :], slot[:, :, :]).then_inc(slots_ready, 1)
                link.done()

            lnx_stats(0)
            ln_apply("x", xt, tn, 0)
            P1(0)
            for s in zeroed:
                dve.wait_ge(s, 16)
            for h in range(H):
                row_max(0, h, x1_full, nm, x1_max, 2)

            def body(i):
                X, Y, Z, W = has(i), has(i - 1), has(i + 1), has(i - 2)
                for h in range(H):
                    if Y:
                        row_max(i - 1, h, y1_full, nm, y1_max, 4)
                    if W and h == 0:
                        dve.wait_ge(free["P3a"], (i - 1) * 2)
                        ln_stats("n2", zk, i - 2)
                    if Z and h == 1:
                        lnx_stats(i + 1)
                    if W and h == 2:
                        if not first(i - 2):
                            dve.wait_ge(st_n2, (i - 2) * 16)
                        ln_apply("n2", zk, n2, i - 2)
                    if X and h >= 2 and h % 2 == 0:
                        xnorm(i, h // 2 - 1)
                    if Z and h == 5:
                        ln_apply("x", xt, tn, i + 1)
                    if W and h == 9:
                        router(i - 2)
                    if W and h == 13:
                        ranks(i - 2)
                if X:
                    xnorm(i, GX - 1)
                if Z:
                    P1(i + 1)
                if X:
                    XO(i)
                for h in range(H):
                    if Z:
                        row_max(i + 1, h, x1_full, nm, x1_max, 2)
                    if X and h == 0:
                        dve.wait_ge(free["XO"], i * 6 + 6)
                        ln_stats("z", xb, i)
                    if X and h == 2:
                        if not first(i):
                            dve.wait_ge(zk_ready, i)
                            dve.wait_ge(xk_ready, i)
                        ln_apply("z", xb, z, i)
                    if X and h == 3:
                        dve.wait_ge(ln_done["z"], i + 1)
                        ln_stats("n1", z, i)
                    if X and h == 5:
                        ln_apply("n1", z, tn, i)
                    if Y and h == 11:
                        ynorm(i - 1, 0)
                if Y:
                    ynorm(i - 1, 1)
                if X:
                    P2(i)
                if Y:
                    P3a(i - 1)

            iterations(dve, body)

            link = Chain(dve, b_link, 27, 0)
            dve.wait_ge(ld_tab, 16)
            dve.wait_ge(ld_tab2, 16)
            dve.wait_ge(pool_b, 3)
            dve.wait_ge(cnt_full, 1)
            link(dve.tensor_copy(cnt[:, :], Dn[1][:, 0:16]))
            link(dve.tensor_copy(tabf[:, :, :], tabs[:, :, :]))
            link(dve.tensor_scalar(spos_i[:, :], spos_i[:, :], C - 1, None, ALU.bitwise_and))
            link(dve.tensor_copy(spos[:, :], spos_i[:, :]))
            link(dve.tensor_tensor(own_e[:, :], own_e[:, :], cnt[0:NI, 0:E], ALU.mult))
            link(dve.tensor_reduce(cnt_own[:, :], own_e[:, :], AX_X, ALU.add))
            link(dve.tensor_scalar(spos[:, :], spos[:, :], cnt_own[:, 0:1], None, ALU.is_lt))
            link(dve.tensor_tensor(tabf[:, 0, :], tabf[:, 0, :], tabf[:, 1, :], ALU.subtract))
            link(dve.tensor_tensor(tabf[:, 0, :], tabf[:, 0, :], spos[:, :], ALU.mult))
            dve.tensor_tensor(tabf[:, 0, :], tabf[:, 0, :], tabf[:, 1, :], ALU.add).then_inc(ids_sel, 1)
            dve.wait_ge(idsT_full, 1)
            dve.tensor_copy(ids_u[:, :], Dn[0][:, 0:NI]).then_inc(ids_ready, 1)

            def gates():
                dve.wait_ge(ld_route, 16)
                Rv = Ra[:, :, :, :].rearrange("p b t c -> p (b t) c")
                r1, r2, f1, f2, v1, v2 = (Rv[:, :, c] for c in range(8, 14))
                dve.tensor_tensor(ex[:, :, :], Rv[:, :, 0:E], over(v1, NT), ALU.subtract).then_inc(exb_in, 1)
                dve.tensor_tensor(bb[2][:, :], v2, v1, ALU.subtract).then_inc(exb_in, 1)
                dve.wait_ge(exb, 2)
                link(dve.tensor_reduce(bb[0][:, :], ex[:, :, :], AX_X, ALU.add))
                link(dve.reciprocal(bb[1][:, :], bb[0][:, :]))
                link(dve.tensor_tensor(bb[2][:, :], bb[2][:, :], bb[1][:, :], ALU.mult))
                link(dve.tensor_tensor(ex[:, :, :], each(desc[:, :], NT), over(f2, NT), ALU.is_equal))
                link(dve.tensor_tensor(ex[:, :, :], ex[:, :, :], each(cnt[:, 0:E], NT), ALU.mult))
                link(dve.tensor_reduce(bb[3][:, :], ex[:, :, :], AX_X, ALU.add))
                link(dve.tensor_tensor(bb[3][:, :], bb[3][:, :], r2, ALU.add))
                link(dve.scalar_tensor_tensor(bb[4][:, :], r1, float(C), bb[1][:, :], ALU.is_lt, ALU.mult))
                link(dve.scalar_tensor_tensor(bb[5][:, :], bb[3][:, :], float(C), bb[2][:, :], ALU.is_lt, ALU.mult))
                link(dve.tensor_tensor(bb[6][:, :], bb[4][:, :], bb[5][:, :], ALU.add))
                link(dve.tensor_scalar(bb[6][:, :], bb[6][:, :], FLT_EPS, None, ALU.max))
                link(dve.reciprocal(bb[7][:, :], bb[6][:, :]))
                link(dve.scalar_tensor_tensor(gate[0][:, :], bb[4][:, :], KEEP, bb[7][:, :], ALU.mult, ALU.mult))
                link(dve.scalar_tensor_tensor(gate[1][:, :], bb[5][:, :], KEEP, bb[7][:, :], ALU.mult, ALU.mult))
                link(dve.tensor_scalar(bb[8][:, :], r1, float(C - 1), float(E * C), ALU.min, ALU.add))
                link(dve.scalar_tensor_tensor(bb[8][:, :], f1, -float(C), bb[8][:, :], ALU.mult, ALU.add))
                link(dve.tensor_copy(gidx[0][:, :], bb[8][:, :]))
                link(dve.tensor_scalar(bb[0][:, :], r2, float(C - 1), float(E * C + C - 1), ALU.min, ALU.subtract))
                link(dve.scalar_tensor_tensor(bb[0][:, :], f2, float(C), bb[0][:, :], ALU.mult, ALU.add))
                dve.tensor_scalar(gidx[1][:, :], bb[0][:, :], -1.0, None, ALU.mult).then_inc(gates_ready, 1)
                link.per = link.n
                link.done()

            def weights(e, e2):
                dve.wait_ge(we_hi, e * 2 + 1)
                dve.tensor_tensor(W1[e2][1][:, :, :], w1s[:, :, :], f32(W1[e2][0][:, :, :]),
                                  ALU.subtract).then_inc(we_lo, 1)
                dve.wait_ge(we_hi, e * 2 + 2)
                dve.tensor_tensor(W2[e2][1][:, :, :], w2s[:, :, :], f32(W2[e2][0][:, :, :]),
                                  ALU.subtract).then_inc(we_lo, 1)

            def xt_split(j, k):
                g, r = j * 8 + k, k % 2
                dve.wait_ge(xtf_ready, g + 1)
                if not (first(j) and k < 2):
                    dve.wait_ge(m1_full, (g - 1) * 4)
                dve.tensor_copy(XT[r][0][:, :, :], XTf[:, :, :]).then_inc(xt_hi, 1)
                dve.wait_ge(xt_hi, g + 1)
                dve.tensor_tensor(XT[r][1][:, :, :], XTf[:, :, :], f32(XT[r][0][:, :, :]),
                                  ALU.subtract).then_inc(xt_ready, 1)

            def hid_lo(j, k):
                g = j * 8 + k
                for c in range(4):
                    dve.wait_ge(h_hi, g * 4 + c + 1)
                    o = slice(2 * c, 2 * c + 2)
                    dve.tensor_tensor(HT_[k % 2][1][:, o, :], hid[c % 2][:, :, :], f32(HT_[k % 2][0][:, o, :]),
                                      ALU.subtract).then_inc(h_ready, 1)

            def y_out(j, k):
                g, r, e2 = j * 8 + k, k % 2, (k // 4) % 2
                dve.wait_ge(m2_full, g + 1)
                if not (first(j) and k < 2):
                    dve.wait_ge(st_y[r], (j * 4 + (k - r) // 2) * 16)
                if k % 4 == 0:
                    dve.wait_ge(ld_b2[e2], (j + (k // 8)) * 16 + 16)
                dve.tensor_tensor(ys[r][:, :, :], bank(YB[r]), b2e[e2][:, :].unsqueeze(1).to_broadcast([P, 2, D]),
                                  ALU.add).then_inc(y_ready, 1)

            weights(0, 0)
            xt_split(0, 0)
            gates()

            def body_c(j):
                for k in range(8):
                    if k % 4 == 1 and not (k == 5 and isinstance(j, int) and j == NG // 8 - 1):
                        weights(j * 2 + k // 4 + 1, 1 - k // 4)
                    if k < 7 or not (isinstance(j, int) and j == NG // 8 - 1):
                        xt_split(j, k + 1) if k < 7 else xt_split(j + 1, 0)
                    hid_lo(j, k)
                    if k or not first(j):
                        y_out(j, k - 1)

            groups(dve, body_c)
            y_out(NG // 8 - 1, 7)

            def body_d(i):
                if not first(i):
                    dve.wait_ge(comb, i * UD)
                for j in range(2):
                    last = dve.tensor_copy(cg[j][:, :], gate[j][:, bass.ds(i * UD, UD)])
                last.then_inc(cg_ready, 1)
                dve.wait_ge(cg_ready, i + 1)
                for k in range(UD):
                    dve.wait_ge(ldb[k], i * 16 + 16)
                    dve.wait_ge(gd[0][k], i * 16 + 16)
                    dve.scalar_tensor_tensor(ba[k][:, :], ya[0][k][:, :], cg[0][:, k:k + 1], ba[k][:, :],
                                             ALU.mult, ALU.add).then_inc(comb_mid, 1)
                    dve.wait_ge(comb_mid, i * UD + k + 1)
                    dve.wait_ge(gd[1][k], i * 16 + 16)
                    dve.scalar_tensor_tensor(ba[k][:, :], ya[1][k][:, :], cg[1][:, k:k + 1], ba[k][:, :],
                                             ALU.mult, ALU.add).then_inc(comb, 1)

            body_d(0)
            with dve.Fori(1, NT // UD) as i:
                body_d(i)

        @blk.gpsimd
        def _(pool):
            n = [0]

            def link(ins):
                n[0] += 1
                ins.then_inc(pool_link, 1)
                hold(pool, pool_link, n[0])

            link(pool.memset(ident[:, :], 0.0))
            link(pool.affine_select(out=ident[:, :], in_=ident[:, :], compare_op=ALU.not_equal, fill=1.0, base=0,
                                    pattern=[[-1, P]], channel_multiplier=1))
            link(pool.memset(upper[:, :], 1.0))
            link(pool.affine_select(out=upper[:, :], in_=upper[:, :], compare_op=ALU.is_gt, fill=0.0, base=0,
                                    pattern=[[1, P]], channel_multiplier=-1))
            link(pool.memset(ones_b[:, :], 1.0))
            pool.memset(macc[:, :], 0.0).then_inc(macc_ready, 1)
            link(pool.memset(neghalf[:, :], -0.5))
            link(pool.memset(Vs[:, :, :, :], 1.0))
            link(pool.memset(R[:, :, :], 0.0))
            few = nm[:, 0, 0:E].bitcast(I32)
            link(pool.iota(few, pattern=[[-1, E]], base=E, channel_multiplier=0))
            link(pool.tensor_copy(desc[:, :], few))
            link(pool.memset(nm[:, :, :], 0.0))
            link(pool.iota(irow[:, :], pattern=[[0, 1]], base=0, channel_multiplier=1))
            link(pool.iota(tok_i[:, :], pattern=[[P, TT]], base=0, channel_multiplier=1))
            link(pool.tensor_copy(tok_f[:, :], tok_i[:, :]))
            pool.memset(neghalf[:, :], -0.5).then_inc(pool_consts, 1)
            hold(pool, pool_consts, 1)
            hold(pool, w_lo, 8)
            pool.memset(Vx[:, :, :, HD:HD + 1], 1.0).then_inc(vx_ones, 1)

            def rsqrt(name, b):
                _, mv, rs = stats[name]
                hold(pool, mv_done[name], b + 1)
                pool.tensor_scalar(rs[:, :], mv[:, :, 1], EPS, None, ALU.add).then_inc(rs_link[name], 1)
                hold(pool, rs_link[name], b + 1)
                pool.tensor_tensor(rs[:, :], rs[:, :], neghalf[:, :], ALU.pow).then_inc(rs_done[name], 1)

            def both(ap):
                return ap[:, :].unsqueeze(1).to_broadcast([P, TT, D])

            hold(pool, ld_small, 16 * SMALL)
            rsqrt("x", 0)

            def scatter(b):
                hold(pool, slots_ready, b + 1)
                if first(b):
                    for s in zeroed:
                        hold(pool, s, 16)
                for t in range(TT):
                    for a in range(2):
                        pool.indirect_dma_start(slot_d[a], bass.IndirectOffsetOnAxis(slot_u[:, t, a:a + 1], 0),
                                                tok_i[:, t:t + 1], None, bounds_check=E * C - 1,
                                                oob_is_err=False).then_inc(scat[2 * t + a], 16)

            def body(i):
                X, Y, Z, W = has(i), has(i - 1), has(i + 1), has(i - 2)
                if W:
                    rsqrt("n2", i - 2)
                if Z:
                    rsqrt("x", i + 1)
                if Y:
                    if W:
                        hold(pool, ln_done["n2"], i - 1)
                        hold(pool, st_base, (i - 1) * 16)
                    hold(pool, ln_done["z"], i)
                    pool.tensor_tensor(zk[:, :, :], z[:, :, :], both(sbo_r), ALU.add).then_inc(zk_ready, 1)
                    pool.tensor_copy(xk[:, :, :], xb[:, :, :]).then_inc(xk_ready, 1)
                if X:
                    hold(pool, ld_r, i * 16 + 16)
                    pool.tensor_tensor(xb[:, :, :], xb[:, :, :], both(bo_r), ALU.add).then_inc(xb_ready, 1)
                if W:
                    scatter(i - 2)
                if X:
                    rsqrt("z", i)
                    rsqrt("n1", i)
                if Y:
                    hold(pool, free["P3a"], i * 2)
                    hold(pool, xk_ready, i)
                    pool.tensor_tensor(xk[:, :, :], zk[:, :, :], xk[:, :, :], ALU.add).then_inc(base_ready, 1)

            iterations(pool, body)

            hold(pool, ld_tab, 16)
            pool.iota(spos_i[:, :], pattern=[[1, P]], base=0, channel_multiplier=P).then_inc(pool_b, 1)
            pool.memset(own_e[:, :], 1.0).then_inc(pool_b2, 1)
            hold(pool, pool_b2, 1)
            pool.affine_select(out=own_e[:, :], in_=own_e[:, :], compare_op=ALU.is_ge, fill=0.0, base=0,
                               pattern=[[-(C // P), E]], channel_multiplier=1).then_inc(pool_b2, 1)
            hold(pool, pool_b2, 2)
            pool.affine_select(out=own_e[:, :], in_=own_e[:, :], compare_op=ALU.is_ge, fill=0.0, base=C // P - 1,
                               pattern=[[C // P, E]], channel_multiplier=-1).then_inc(pool_b, 2)

            def gather(j, k):
                g, r = j * 8 + k, k % 2
                if not (first(j) and k < 2):
                    hold(pool, cx_full, g - 1)
                pool.tensor_copy(gi[r][:, :], ids_u[:, bass.ds(j * 16 + 2 * k, 2)]).then_inc(gi_ready, 1)
                hold(pool, gi_ready, g + 1)
                for q in range(2):
                    pool.indirect_dma_start(Xg[r][:, q, :], None, n2_d, bass.IndirectOffsetOnAxis(gi[r][:, q:q + 1], 0),
                                            bounds_check=T - 1, oob_is_err=False).then_inc(gath[r][q], 16)

            def hid_hi(j, k):
                g = j * 8 + k
                for c in range(4):
                    hold(pool, relu_done, g * 4 + c + 1)
                    if c == 0 and not (first(j) and k < 2):
                        hold(pool, m2_full, g - 1)
                    pool.tensor_copy(HT_[k % 2][0][:, 2 * c:2 * c + 2, :], hid[c % 2][:, :, :]).then_inc(h_hi, 1)

            hold(pool, ids_ready, 1)
            gather(0, 0)
            gather(0, 1)

            def body_c(j):
                for k in range(8):
                    hid_hi(j, k)
                    if k < 6:
                        gather(j, k + 2)
                    elif not (isinstance(j, int) and j == NG // 8 - 1):
                        gather(j + 1, k - 6)

            groups(pool, body_c)

            for s in st_y:
                hold(pool, s, NG // 2 * 16)
            hold(pool, gates_ready, 1)
            with pool.Fori(0, NT // UD) as i:
                for j in range(2):
                    pool.tensor_copy(ci[j][:, :], gidx[j][:, bass.ds(i * UD, UD)]).then_inc(ciq, 1)
                hold(pool, ciq, i * 2 + 2)
                for k in range(UD):
                    for j in range(2):
                        pool.indirect_dma_start(ya[j][k][:, :], None, y_d,
                                                bass.IndirectOffsetOnAxis(ci[j][:, k:k + 1], 0),
                                                bounds_check=E * C - 1, oob_is_err=False).then_inc(gd[j][k], 16)
                hold(pool, comb, i * UD + UD)

        @blk.sync
        def _(sp):
            def small(dst, src):
                sp.dma_start(dst, src, allow_slow_non_contiguous=True).then_inc(ld_small, 16)
                count[0] += 1

            count = [0]

            def rows(a, b):
                return a[b, :, :].rearrange("(t p) d -> p t d", p=P) if isinstance(b, int) else \
                    a[bass.ds(b, 1), :, :].rearrange("a (t p) d -> p (a t) d", p=P)

            def tokens(a, b):
                return rows(a.rearrange("(b s) d -> b s d", s=S), b)

            def load_x(b):
                sp.dma_start(xt[:, :, :], rows(x, b)).then_inc(ld_x, 16)

            def load_c(b):
                sp.dma_start(ct[:, :, :], rows(ctx, b)).then_inc(ld_c, 16)

            def load_r(b):
                sp.dma_start(xb[:, :, :], rows(x, b)).then_inc(ld_r, 16)

            load_x(0)
            load_c(0)
            for n, ((dst, src), _) in enumerate(weight_parts):
                if n == 7:
                    sp.wait_ge(w_lo, 1)
                sp.dma_start(dst, src).then_inc(ld_w[n], 16)
            small(bqc[:, :], bq.rearrange("(t a) d -> (a d) t", a=2))
            small(bkc[:, :], bk.rearrange("(t a) d -> (a d) t", a=2))
            small(bv_r[:, :], bv.rearrange("h d -> (h d)").partition_broadcast(P))
            small(bo_r[:, :], bo.partition_broadcast(P))
            small(sbv_r[:, :], sbv.partition_broadcast(P))
            small(sbo_r[:, :], sbo.partition_broadcast(P))
            for src, dst in ((sbq, sbqc), (sbk, sbkc)):
                v = src.rearrange("(t j r) -> j r t", j=4, r=SD)
                for j in range(4):
                    for s in range(2):
                        small(dst[32 * j + SD * s:32 * j + SD * s + SD, :], v[j])
            for src, dst in ((g1, g1c), (b1n, b1c), (g2, g2c), (b2n, b2c)):
                small(dst[:, :], src.rearrange("(k p) -> p k", p=P))
            small(wrs[:, :, :], wr.rearrange("(k p) e -> p k e", p=P))
            assert count[0] == SMALL, count[0]
            sp.wait_ge(pool_consts, 1)
            for a in range(2):
                sp.dma_start(slot_d[a].rearrange("(p c) a -> p (c a)", p=P), nm[:, 0, 0:E * C // P].bitcast(I32)).then_inc(zeroed[a], 16)
            load_r(0)
            sp.wait_ge(ln_done["x"], 1)
            load_x(1)
            sp.wait_ge(full["P1"], 2)
            load_c(1)

            def body(i):
                X, Y, W = has(i), has(i - 1), has(i - 2)
                if W:
                    sp.wait_ge(ln_done["n2"], i - 1)
                    sp.dma_start(tokens(n2_d, i - 2), n2[:, :, :]).then_inc(st_n2, 16)
                if Y and X:
                    sp.wait_ge(xk_ready, i)
                    load_r(i)
                if has(i + 2):
                    sp.wait_ge(ln_done["x"], i + 2)
                    load_x(i + 2)
                if W:
                    sp.wait_ge(slots_ready, i - 1)
                    sp.dma_start(route_d[i - 2] if isinstance(i, int) else
                                 route_d[bass.ds(i - 2, 1), :, :].rearrange("a p c -> (a p) c"),
                                 R[:, :, :].rearrange("p t c -> p (t c)")).then_inc(st_r, 16)
                if has(i + 2):
                    sp.wait_ge(full["P1"], (i + 1) * 14 + 2)
                    load_c(i + 2)
                if Y:
                    sp.wait_ge(base_ready, i)
                    sp.dma_start(tokens(base_d, i - 1), xk[:, :, :]).then_inc(st_base, 16)

            def iterations_sp():
                body(0), body(1)
                with sp.Fori(2, B - 2) as i:
                    body(i)
                body(B - 2), body(B - 1), body(B), body(B + 1)

            iterations_sp()

            for s in (st_base, st_n2, st_r, *scat):
                sp.wait_ge(s, B * 16)
            sp.wait_ge(cnt_full, 1)
            for a in range(2):
                sp.dma_start(tabs[:, a, :], slot_d[a].rearrange("(n p) a -> n (p a)", p=P)).then_inc((ld_tab, ld_tab2)[a], 16)
            sp.dma_start(Ra[:, :, :, :].rearrange("p b t c -> p b (t c)"),
                         route_d.rearrange("b p c -> p b c")).then_inc(ld_route, 16)

            def at(a, e, pattern):
                return a[bass.ds(e, 1)].rearrange(pattern, p=P) if not isinstance(e, int) else \
                    a[e:e + 1].rearrange(pattern, p=P)

            def load_expert(e, e2):
                if not first(e):
                    sp.wait_ge(we_lo, e * 2 - 1)
                sp.dma_start(w1s[:, :, :], at(w1, e, "a (k p) f -> p (a k) f")).then_inc(ld_w1, 16)
                if not first(e):
                    sp.wait_ge(we_lo, e * 2)
                sp.dma_start(w2s[:, :, :], at(w2, e, "a (f p) d -> p (a f) d")).then_inc(ld_w2, 16)
                if not first(e, 2):
                    sp.wait_ge(y_ready, (e - 1) * 4)
                sp.dma_start(b1e[e2][:, :], at(b1, e, "a (f p) -> p (a f)"), allow_slow_non_contiguous=True)\
                    .then_inc(ld_b1[e2], 16)
                sp.dma_start(b2e[e2][:, :], (b2[e] if isinstance(e, int) else
                                             b2[bass.ds(e, 1), :].rearrange("a d -> (a d)")).partition_broadcast(P))\
                    .then_inc(ld_b2[e2], 16)

            def store_y(j, k):
                g, r = j * 8 + k, k % 2
                sp.wait_ge(y_ready, g + 1)
                yv = y_d.rearrange("(g q p) d -> g p q d", q=2, p=P)
                sp.dma_start(yv[bass.ds(g, 1)].rearrange("a p q d -> p (a q) d") if not isinstance(g, int) else yv[g],
                             ys[r][:, :, :]).then_inc(st_y[r], 16)

            load_expert(0, 0)
            load_expert(1, 1)

            def body_c(j):
                for k in range(8):
                    store_y(j, k)
                    if k % 4 == 2 and not (isinstance(j, int) and j == NG // 8 - 1):
                        load_expert(j * 2 + 2 + k // 4, k // 4)

            groups(sp, body_c)

            def base_tile(i, k):
                v = base_d.rearrange("(i k p) d -> i k p d", k=UD, p=P)
                return v[bass.ds(i, 1), k].rearrange("a p d -> (a p) d") if not isinstance(i, int) else v[i, k]

            def out_tile(i, k):
                v = out.rearrange("b s d -> (b s) d").rearrange("(i k p) d -> i k p d", k=UD, p=P)
                return v[bass.ds(i, 1), k].rearrange("a p d -> (a p) d") if not isinstance(i, int) else v[i, k]

            for k in range(UD):
                sp.dma_start(ba[k][:, :], base_tile(0, k)).then_inc(ldb[k], 16)

            def store_out(i, k):
                sp.wait_ge(comb, i * UD + k + 1)
                sp.dma_start(out_tile(i, k), ba[k][:, :]).then_inc(sto[k], 16)

            with sp.Fori(0, NT // UD - 1) as i:
                for k in range(UD):
                    store_out(i, k)
                for k in range(UD):
                    sp.wait_ge(sto[k], i * 16 + 16)
                    sp.dma_start(ba[k][:, :], base_tile(i + 1, k)).then_inc(ldb[k], 16)
            for k in range(UD):
                store_out(NT // UD - 1, k)
            for k in range(UD):
                sp.wait_ge(sto[k], NT // UD * 16)


_INS = ['x', 'ctx_1024', 'L0_xattn_Wq', 'L0_xattn_bq', 'L0_xattn_Wk', 'L0_xattn_bk', 'L0_xattn_Wv', 'L0_xattn_bv',
        'L0_xattn_Wo', 'L0_xattn_bo', 'L0_ffn_wq', 'L0_ffn_bq', 'L0_ffn_wk', 'L0_ffn_bk', 'L0_ffn_wv', 'L0_ffn_bv',
        'L0_ffn_wo', 'L0_ffn_bo', 'L0_ffn_ln1_g', 'L0_ffn_ln1_b', 'L0_ffn_ln2_g', 'L0_ffn_ln2_b', 'L0_ffn_wr',
        'L0_ffn_w1', 'L0_ffn_b1', 'L0_ffn_w2', 'L0_ffn_b2']


def kernel(**inputs):
    import numpy as np
    import concourse.bacc as bacc
    from concourse.bass_utils import run_bass_kernel_spmd

    nc = bacc.Bacc("TRN2", target_bir_lowering=False, num_devices=1)
    arrays, args = {}, []
    for name in _INS:
        a = np.ascontiguousarray(inputs[name])
        arrays[f"in_{name}"] = a
        args.append(nc.dram_tensor(f"in_{name}", a.shape, mybir.dt.from_np(a.dtype), kind="ExternalInput").ap())
    shape = arrays["in_x"].shape
    out = nc.dram_tensor("out_rows", shape, F32, kind="ExternalOutput").ap()
    xattn_moe(nc, *args, out)
    r = run_bass_kernel_spmd(nc, [arrays], core_ids=[0])
    return r.results[0]["out_rows"]
```

```python
from contextlib import ExitStack

import concourse.bass as bass
from concourse import mybir

F32 = mybir.dt.float32
F32R = mybir.dt.float32r
BF16 = mybir.dt.bfloat16
I32 = mybir.dt.int32
U32 = mybir.dt.uint32
ALU = mybir.AluOpType
ACT = mybir.ActivationFunctionType
AX_X = mybir.AxisListType.X

P = 128
EPS = 1e-5
FLT_EPS = 1.1920928955078125e-07
FAR = 1048576.0


def xattn_moe(nc, x, ctx, Wq, bq, Wk, bk, Wv, bv, Wo, bo, swq, sbq, swk, sbk, swv, sbv, swo, sbo,
              g1, b1n, g2, b2n, wr, w1, b1, w2, b2, out):
    B, S, D = x.shape
    _, H, HD = Wq.shape
    E, _, F = w1.shape
    T = B * S
    C = -(-T // 4)
    KD, TT = D // P, S // P
    HT = H * HD // P
    SD = D // H
    GX, GY = H // 2, H // 4
    FT = F // P
    XS, YS = float(HD) ** -0.5, float(SD) ** -0.5
    KEEP = 0.8
    assert S == 256 and D == 256 and HD == 64 and SD == 16 and H == 16 and E == 8 and C == 1024

    base_d = nc.dram_tensor("base_rows", (T, D), F32).ap()
    n2_d = nc.dram_tensor("n2_rows", (T, D), F32).ap()
    y_d = nc.dram_tensor("y_rows", (E * C, D), F32).ap()
    route_d = nc.dram_tensor("route_rows", (B, P, TT * 16), F32).ap()
    qk_d = [nc.dram_tensor(f"self_{n}_rows", (H, 3, SD, S), F32).ap() for n in "qk"]
    slot_d = [nc.dram_tensor(f"slot_tokens_{j}", (E * C, 1), I32).ap() for j in range(2)]

    whole = ExitStack()
    with whole:
        def sem(name):
            return whole.enter_context(nc.semaphore(name))

        def psum(name):
            return whole.enter_context(nc.psum_tensor(name, [P, 512], F32))

        def keep(name, shape, dt=F32):
            return whole.enter_context(nc.sbuf_tensor(name, shape, dt))

        Sp = [psum(f"scoresT{k}") for k in range(2)]
        Sn = [psum(f"scores{k}") for k in range(2)]
        Op = [psum(f"attn_out{k}") for k in range(2)]
        Dn = [psum(f"dense{k}") for k in range(2)]

        ident = keep("ident", [P, P])
        macc = keep("mask_totals", [P, 16], BF16)
        ones_b = keep("ones_b", [P, P], BF16)
        upper = keep("upper_b", [P, P], BF16)
        desc = keep("desc", [P, E])
        g2c, b2c = keep("g2c", [P, KD]), keep("b2c", [P, KD])

        part_a = ExitStack()

        def sa(name, shape, dt=F32):
            return part_a.enter_context(nc.sbuf_tensor(name, shape, dt))

        def pair(name, shape):
            return sa(name + "_hi", shape, F32R), sa(name + "_lo", shape, F32R)

        Wqs, Wks, Wvs = (pair(n, [P, KD, H * HD]) for n in ("Wq", "Wk", "Wv"))
        Wos = pair("Wo", [P, HT, D])
        swqs, swks, swvs, swos = (pair(n, [P, KD, D]) for n in ("swq", "swk", "swv", "swo"))
        QT, KT = pair("QT", [P, HT, S]), pair("KT", [P, HT, S])
        Vx = sa("Vx", [P, TT, H, HD + 1])
        U = sa("transposed", [P, 16, S], F32R)
        OT = U[:, 0:8, :], U[:, 8:16, :]
        zT = U[:, 0:2, :], U[:, 2:4, :]
        cT = U[:, 4:6, :], U[:, 6:8, :]
        nT = U[:, 8:10, :], U[:, 10:12, :]
        O2T = U[:, 12:14, :], U[:, 14:16, :]
        O = sa("O", [P, TT, H * HD])
        PT = sa("PT", [P, 4, TT * S])
        SQ, SK = sa("self_q", [P, HT, S], F32R), sa("self_k", [P, HT, S], F32R)
        Vs = sa("Vs", [P, TT, H, 2 * SD])
        OY = sa("self_out_T", [P, 2, S])
        O2 = sa("O2", [P, TT, D])
        tf = sa("affine_T", [P, KD, S])
        xt, ct, tn, xb, z, zk, xk, n2 = (sa(n, [P, TT, D]) for n in
                                         ("xt", "ct", "tn", "xb", "z", "zk", "xk", "n2"))
        q_parts, k_parts = (U[:, 0:2, :], U[:, 2:4, :]), (U[:, 4:6, :], U[:, 6:8, :])
        bv_r, bo_r, sbv_r, sbo_r = sa("bv_r", [P, H * HD]), sa("bo_r", [P, D]), sa("sbv_r", [P, D]), sa("sbo_r", [P, D])
        bqc, bkc = sa("bqc", [P, HT]), sa("bkc", [P, HT])
        sbqc, sbkc = sa("sbqc", [P, KD]), sa("sbkc", [P, KD])
        g1c, b1c = sa("g1c", [P, KD]), sa("b1c", [P, KD])
        wrs = sa("wrs", [P, KD, E])
        nm = sa("neg_max", [P, TT, P])
        mT = sa("neg_max_T", [P, S], F32R)
        pick_x = sa("pick_x", [P, HT], F32R)
        neghalf = sa("neghalf", [P, TT])
        rcx, rcy = sa("rcx", [P, 2, 4]), sa("rcy", [P, 2, H])
        stats = {n: (sa(f"st_{n}", [P, TT, 6]), sa(f"mv_{n}", [P, TT, 2]), sa(f"rs_{n}", [P, TT]))
                 for n in ("x", "z", "n1", "n2")}
        R = sa("route", [P, TT, 16])
        eq = sa("eq", [P, TT, E])
        m1, L2 = sa("m1", [P, TT, E]), sa("L2", [P, TT, E])
        M = sa("masks", [P, TT, 2, E], BF16)
        mr = sa("masked_ranks", [P, TT, 2, E])
        slot = sa("slot", [P, TT, 2])
        oob = sa("oob", [P, TT, 2])
        slot_u = sa("slot_u", [P, TT, 2], U32)
        tok_f = sa("tok_f", [P, TT])
        tok_i = sa("tok_i", [P, TT], I32)
        part_a.close()

        part_c = ExitStack()

        def sc(name, shape, dt=F32):
            return part_c.enter_context(nc.sbuf_tensor(name, shape, dt))

        w1s, w2s = sc("w1s", [P, KD, F]), sc("w2s", [P, FT, D])
        W1 = [(sc(f"W1h{k}", [P, KD, F], F32R), sc(f"W1l{k}", [P, KD, F], F32R)) for k in range(2)]
        W2 = [(sc(f"W2h{k}", [P, FT, D], F32R), sc(f"W2l{k}", [P, FT, D], F32R)) for k in range(2)]
        b1e = [sc(f"b1e{k}", [P, FT]) for k in range(2)]
        b2e = [sc(f"b2e{k}", [P, D]) for k in range(2)]
        Xg = [sc(f"Xg{k}", [P, 2, D]) for k in range(2)]
        XTf = sc("XTf", [P, KD, 256])
        XT = [(sc(f"XTh{k}", [P, KD, 256], F32R), sc(f"XTl{k}", [P, KD, 256], F32R)) for k in range(2)]
        hid = [sc(f"hid{k}", [P, 2, 256]) for k in range(2)]
        HT_ = [(sc(f"Hh{k}", [P, FT, 256], F32R), sc(f"Hl{k}", [P, FT, 256], F32R)) for k in range(2)]
        ys = [sc(f"ys{k}", [P, 2, D]) for k in range(2)]
        gi = [sc(f"gi{k}", [P, 2], U32) for k in range(2)]
        NT = T // P
        Ra = sc("route_all", [P, B, TT, 16])
        NI = E * C // P
        tabs, tabf = sc("tabs", [NI, 2, P], I32), sc("tabf", [NI, 2, P])
        spos_i, spos = sc("spos_i", [NI, P], I32), sc("spos", [NI, P])
        own_e, cnt_own = sc("own_e", [NI, E]), sc("cnt_own", [NI, 1])
        cnt = sc("cnt", [P, 2 * E])
        ids_u = sc("ids_u", [P, NI], U32)
        ex = sc("ex", [P, NT, E])
        bb = [sc(f"bb{k}", [P, NT]) for k in range(9)]
        gidx = [sc(f"gidx{j}", [P, NT], U32) for j in range(2)]
        gate = [sc(f"gate{j}", [P, NT]) for j in range(2)]
        UD = 8
        ya = [[sc(f"ya{j}_{k}", [P, UD, D]) for k in range(2)] for j in range(2)]
        ba = [sc(f"ba{k}", [P, UD, D]) for k in range(2)]
        part_c.close()

        ld_w = [sem(f"ld_wt{k}") for k in range(8)]
        ld_small, ld_x, ld_c, ld_r = sem("ld_small"), sem("ld_x"), sem("ld_c"), sem("ld_r")
        w_hi, w_lo = sem("w_hi"), sem("w_lo")
        pool_consts, consts = sem("pool_consts"), sem("consts")
        zeroed = [sem("table0_zeroed"), sem("table1_zeroed")]
        mv_done = {n: sem(f"mv_{n}") for n in ("x", "z", "n1", "n2")}
        rs_done = {n: sem(f"rs_{n}") for n in ("x", "z", "n1", "n2")}
        rs_link = {n: sem(f"rs_link_{n}") for n in ("x", "z", "n1", "n2")}
        bn_link = {n: sem(f"bn_link_{n}") for n in ("x", "z", "n1", "n2")}
        ln_done = {n: sem(f"ln_{n}") for n in ("x", "z", "n1", "n2")}
        N = {"P1": 14, "XO": 6, "P2": 4, "P3a": 2, "P3b": 2}
        full = {n: sem(f"full_{n}") for n in N}
        hi = {n: sem(f"hi_{n}") for n in N}
        free = {n: sem(f"free_{n}") for n in N}
        x1_full, y1_full = sem("x1_full"), sem("y1_full")
        x1_max, y1_max = sem("x1_max"), sem("y1_max")
        negx_full, negy_full = sem("negx_full"), sem("negy_full")
        negx, negy = sem("negx"), sem("negy")
        x2_full, y2_full = sem("x2_full"), sem("y2_full")
        x2_exp, y2_exp = sem("x2_exp"), sem("y2_exp")
        x2_av, y2_av = sem("x2_av"), sem("y2_av")
        rec_x, rec_y = sem("rec_x"), sem("rec_y")
        oy_out, oyt_full = sem("oy_out"), sem("oyt_full")
        xo_norm, yo_norm = sem("xo_norm"), sem("yo_norm")
        xb_ready, zk_ready, xk_ready, base_ready = sem("xb_ready"), sem("zk_ready"), sem("xk_ready"), sem("base_ready")
        st_base, st_n2, st_r = sem("st_base"), sem("st_n2"), sem("st_r")
        qk_stored, qk_placed = ([sem(f"{what}_{n}") for n in "qk"] for what in ("stored", "placed"))
        shift_placed = sem("shift_placed")
        tf_ready = sem("tf_ready")
        t2_full, h2_ready = sem("t2_full"), sem("h2_ready")
        route_link, masks_ready, macc_ready = sem("route_link"), sem("masks_ready"), sem("macc_ready")
        slots_ready, route_ready = sem("slots_ready"), sem("route_ready")
        scattered = sem("scattered")

        def split(src, w):
            return [(src, w[0], w[1])]

        def wide(buf):
            return buf.rearrange("p (k n) -> p k n", k=KD)

        vx_flat = Vx[:, :, :, :].rearrange("p t h d -> p (t h d)")[:, 0:KD * H * HD]
        pt_flat = PT[:, :, :].rearrange("p a b -> p (a b)")
        o_flat = O[:, :, :].rearrange("p a b -> p (a b)")

        def by_row(w):
            return w.rearrange("(k p) n -> p k n", p=P)

        weight_parts = [
            ((O[:, :, :], by_row(Wq.rearrange("m h d -> m (h d)"))), split(O[:, :, :], [m[:, :, :] for m in Wqs])),
            ((wide(vx_flat), by_row(Wk.rearrange("m h d -> m (h d)"))), split(wide(vx_flat), [m[:, :, :] for m in Wks])),
            ((wide(pt_flat), by_row(Wv.rearrange("m h d -> m (h d)"))), split(wide(pt_flat), [m[:, :, :] for m in Wvs])),
            ((zk[:, :, :], by_row(swq)), split(zk[:, :, :], [m[:, :, :] for m in swqs])),
            ((z[:, :, :], by_row(swk)), split(z[:, :, :], [m[:, :, :] for m in swks])),
            ((xk[:, :, :], by_row(swv)), split(xk[:, :, :], [m[:, :, :] for m in swvs])),
            ((n2[:, :, :], by_row(swo)), split(n2[:, :, :], [m[:, :, :] for m in swos])),
            ((o_flat.rearrange("p (t n) -> p t n", n=D), by_row(Wo.rearrange("h d n -> (h d) n"))),
             split(o_flat.rearrange("p (t n) -> p t n", n=D), [m[:, :, :] for m in Wos])),
        ]
        SMALL = 13

        blk = whole.enter_context(nc.Block())

        def first(b, n=1):
            return isinstance(b, int) and b < n

        def hold(eng, s, value):
            eng.wait_ge(s, value)
            if not isinstance(value, int):
                eng.nop(nofuse=True)

        class Chain:

            def __init__(self, eng, s, per, b):
                self.eng, self.s, self.at, self.per, self.n = eng, s, b * per, per, 0

            def __call__(self, ins):
                self.n += 1
                ins.then_inc(self.s, 1)
                self.eng.wait_ge(self.s, self.at + self.n)

            def done(self):
                assert self.n == self.per, self.n

        def iterations(eng, body):
            body(0), body(1)
            with eng.Fori(2, B - 1) as i:
                body(i)
            body(B - 1), body(B), body(B + 1)

        def has(b):
            return not isinstance(b, int) or 0 <= b < B

        ORDER = [("P1", 1), ("XO", 0), ("P3b", -2), ("P3a", -1), ("P2", 0)]

        def wait_dense(eng, stage, b):
            k = [s for s, _ in ORDER].index(stage)
            i = b - ORDER[k][1]
            while True:
                k -= 1
                if k < 0:
                    k, i = len(ORDER) - 1, i - 1
                s, off = ORDER[k]
                if isinstance(i, int) and i < -1:
                    return
                if has(i + off) and not (isinstance(i, int) and i == -1 and s != "P1"):
                    eng.wait_ge(free[s], (i + off) * N[s] + N[s])
                    return

        def bank(ps, n=2):
            return ps[:, :].rearrange("p (a c) -> p a c", a=n)

        P1_JOBS = [("T", 0), ("T", 1), ("q", 0), ("k", 0), ("q", 1), ("k", 1), ("v", 0, 0), ("v", 1, 0),
                   ("q", 2), ("k", 2), ("q", 3), ("k", 3), ("v", 0, 1), ("v", 1, 1)]
        P1_AT = {4: (0, 1), 5: (2,), 6: (3,), 8: (4,), 9: (5,), 10: (6,), 11: (7,), 12: (8,), 13: (9,),
                 16: (10,), 17: (11,)}
        P1_LAST = (12, 13)
        P3B_AT = (8, 10, 14)
        P1_HI = [n for n, j in enumerate(P1_JOBS) if j[0] != "v"]
        XO_AT = (0, 1, 2, 3, 4, 5, 6, 7)
        STEPS_C = H + 3
        LAG = 6
        STEPS_A = H + LAG

        def three(pe, outp, lhs, rhs, a, b, start, stop):
            pe.matmul(outp, a(lhs[0]), b(rhs[0]), start=start, stop=False)
            pe.matmul(outp, a(lhs[1]), b(rhs[0]), start=False, stop=False)
            return pe.matmul(outp, a(lhs[0]), b(rhs[1]), start=False, stop=stop)

        def pe_transpose_in(pe, src, dst):
            for t in range(TT):
                for k in range(KD):
                    last = pe.transpose(bank(dst)[:, k, t * P:(t + 1) * P], src[:, t, k * P:(k + 1) * P], ident[:, :])
            return last

        def pe_project(pe, stage, b, job, w, act_t, t0):
            for j in range(2):
                for k in range(KD):
                    last = three(pe, bank(Dn[job % 2])[:, j, :], w, act_t,
                                 lambda m, k=k, j=j: m[:, k, (t0 + j) * P:(t0 + j + 1) * P],
                                 lambda m, k=k: m[:, k, :], k == 0, k == KD - 1)
            last.then_inc(full[stage], 1)

        def pe_P1(pe, b, jobs):
            for job in jobs:
                if job == 0:
                    wait_dense(pe, "P1", b)
                    pe.wait_ge(ln_done["x"], b + 1)
                elif job == 1:
                    pe.wait_ge(ld_c, (b + 1) * 16)
                else:
                    pe.wait_ge(free["P1"], b * 14 + job - 1)
                if first(b) and job in (2, 3, 6):
                    pe.wait_ge(w_lo, {2: 1, 3: 2, 6: 3}[job])
                kind, n = P1_JOBS[job][:2]
                if kind == "T":
                    pe_transpose_in(pe, (tn, ct)[n], Dn[n]).then_inc(full["P1"], 1)
                elif kind in "qk":
                    pe_project(pe, "P1", b, job, *((Wqs, zT) if kind == "q" else (Wks, cT)), 2 * n)
                else:
                    half = P1_JOBS[job][2]
                    for k in range(KD):
                        last = three(pe, Dn[job % 2][:, :], cT, Wvs, lambda m: m[:, k, n * P:(n + 1) * P],
                                     lambda m: m[:, k, half * 512:(half + 1) * 512], k == 0, k == KD - 1)
                    last.then_inc(full["P1"], 1)

        def pe_X1(pe, b, h):
            rows, t = slice(64 * (h % 2), 64 * (h % 2) + 64), h // 2
            if h == 0:
                pe.wait_ge(free["P1"], b * 14 + 12)
            if h >= 2:
                pe.wait_ge(x1_max, b * H + h - 1)
            elif not first(b, 2):
                pe.wait_ge(negy, b - 1)
            elif b == 1 and h == 0:
                pe.wait_ge(negx, 1)
            for q in range(TT):
                last = pe.matmul(bank(Sn[h % 2])[:, q, :], QT[0][rows, t, q * P:(q + 1) * P], KT[0][rows, t, :],
                                 start=True, stop=True)
            last.then_inc(x1_full, 1)

        def pe_Y1(pe, b, h):
            rows, t = slice(64 * (h % 2), 64 * (h % 2) + 3 * SD), h // 2
            if h == 0:
                for placed in qk_placed:
                    pe.wait_ge(placed, b * 32 + 32)
            if h >= 2:
                pe.wait_ge(y1_max, b * H + h - 1)
            elif h == 0:
                pe.wait_ge(negx, b + 2 if has(b + 1) else b + 1)
            for q in range(TT):
                last = pe.matmul(bank(Sn[h % 2])[:, q, :], SQ[rows, t, q * P:(q + 1) * P], SK[rows, t, :],
                                 start=True, stop=True)
            last.then_inc(y1_full, 1)

        def pe_neg(pe, b, done, s):
            pe.wait_ge(done, b * H + H)
            for q in range(TT):
                last = pe.transpose(Sn[0][:, q * P:(q + 1) * P], nm[:, q, :], ident[:, :])
            last.then_inc(s, 1)

        def scores_free(pe, b, h, mine, cross):
            if h >= 2:
                pe.wait_ge(mine, b * H + h - 1)
            elif cross:
                if not first(b, 2):
                    pe.wait_ge(y2_exp, (b - 1) * H)
                elif b == 1:
                    pe.wait_ge(x2_exp, H)
            else:
                if has(b + 1):
                    pe.wait_ge(x2_exp, (b + 2) * H)
                else:
                    pe.wait_ge(y2_exp, b * H)

        def pe_X2(pe, b, h):
            rows, t = slice(64 * (h % 2), 64 * (h % 2) + 64), h // 2
            if h == 0:
                pe.wait_ge(negx, b + 1)
            scores_free(pe, b, h, x2_exp, True)
            for k in range(TT):
                o = bank(Sp[h % 2])[:, k, :]
                three(pe, o, KT, QT, lambda m: m[rows, t, k * P:(k + 1) * P], lambda m: m[rows, t, :], True, False)
                last = pe.matmul(o, pick_x[rows, t:t + 1].to_broadcast([64, P]), mT[rows, :], start=False, stop=True)
            last.then_inc(x2_full, 1)

        def pe_Y2(pe, b, h):
            rows, t = slice(64 * (h % 2), 64 * (h % 2) + 3 * SD + 1), h // 2
            if h == 0:
                pe.wait_ge(shift_placed, b * 32 + 32)
            scores_free(pe, b, h, y2_exp, False)
            for k in range(TT):
                last = pe.matmul(bank(Sp[h % 2])[:, k, :], SK[rows, t, k * P:(k + 1) * P], SQ[rows, t, :],
                                 start=True, stop=True)
            last.then_inc(y2_full, 1)

        def pe_XAV(pe, b, h):
            g, hh = divmod(h, 2)
            if h == 0:
                pe.wait_ge(free["P1"], b * 14 + 14)
                if first(b):
                    pe.wait_ge(vx_ones, 1)
            if hh == 0:
                if g >= 2:
                    pe.wait_ge(xo_norm, b * GX + g - 1)
                elif not first(b, 2):
                    pe.wait_ge(yo_norm, (b - 1) * GY)
                elif b == 1:
                    pe.wait_ge(xo_norm, GX)
            pe.wait_ge(x2_exp, b * H + h + 1)
            o = Op[g % 2][:, 0:TT * 2 * (HD + 1)].rearrange("p (q a c) -> p q a c", q=TT, a=2)
            for q in range(TT):
                for k in range(TT):
                    last = pe.matmul(o[:, q, hh, :], PT[:, h % 4, k * S + q * P:k * S + (q + 1) * P], Vx[:, k, h, :],
                                     start=k == 0, stop=k == TT - 1)
            last.then_inc(x2_av, 1)

        def pe_YAV(pe, b, h):
            g, j = divmod(h, 4)
            if h == 0:
                pe.wait_ge(free["P2"], b * 4 + 4)
            if j == 0:
                if g >= 2:
                    pe.wait_ge(yo_norm, b * GY + g - 1)
                elif has(b + 1):
                    pe.wait_ge(xo_norm, (b + 2) * GX)
                else:
                    pe.wait_ge(yo_norm, b * GY)
            pe.wait_ge(y2_exp, b * H + h + 1)
            for k in range(TT):
                last = pe.matmul(Op[g % 2][32 * j:32 * j + 32, 0:S], Vs[:, k, h, :], PT[:, h % 4, k * S:(k + 1) * S],
                                 start=k == 0, stop=k == TT - 1)
            last.then_inc(y2_av, 1)

        def pe_YT(pe, b, g):
            pe.wait_ge(oy_out, b * GY + g + 1)
            for q in range(TT):
                last = pe.transpose(bank(Op[g % 2])[:, 1, q * P:(q + 1) * P], OY[:, g % 2, q * P:(q + 1) * P],
                                    ident[:, :])
            last.then_inc(oyt_full, 1)

        def pe_XO(pe, b, step):
            if step == 0:
                wait_dense(pe, "XO", b)
            if step < 4:
                if step >= 2:
                    pe.wait_ge(free["XO"], b * 6 + step - 1)
                pe.wait_ge(xo_norm, b * GX + 2 * step + 2)
                for j in range(2):
                    for q in range(TT):
                        t = 2 * step + j
                        last = pe.transpose(bank(Dn[step % 2])[:, j, q * P:(q + 1) * P], O[:, q, t * P:(t + 1) * P],
                                            ident[:, :])
                last.then_inc(full["XO"], 1)
            else:
                if step == 4:
                    pe.wait_ge(free["XO"], b * 6 + 4)
                q, half = divmod(step - 4, 2)
                for t in range(half * HT // 2, (half + 1) * HT // 2):
                    last = three(pe, Dn[q][:, 0:D], OT, Wos, lambda m: m[:, t, q * P:(q + 1) * P],
                                 lambda m: m[:, t, :], t == 0, t == HT - 1)
                if half:
                    last.then_inc(full["XO"], 1)

        def pe_P2_P3a(pe, i, X, Y, Z):
            b = i - 1
            if X or Y:
                wait_dense(pe, "P3a", b)
            if X:
                pe.wait_ge(ln_done["n1"], i + 1)
                pe_transpose_in(pe, tn, Dn[0]).then_inc(full["P2"], 1)
            if Z:
                pe_neg(pe, i + 1, x1_max, negx_full)
            if Y:
                pe.wait_ge(yo_norm, b * GY + GY)
                pe_transpose_in(pe, O2, Dn[1]).then_inc(full["P3a"], 1)
                pe.wait_ge(free["P3a"], b * 2 + 1)
            if X:
                pe.wait_ge(free["P2"], i * 4 + 1)
                pe_project(pe, "P2", i, 1, swqs, nT, 0)
                pe_project(pe, "P2", i, 2, swks, nT, 0)
                pe.wait_ge(free["P2"], i * 4 + 2)
            if Y:
                for q in range(TT):
                    for t in range(KD):
                        last = three(pe, bank(Dn[1])[:, q, :], O2T, swos, lambda m: m[:, t, q * P:(q + 1) * P],
                                     lambda m: m[:, t, :], t == 0, t == KD - 1)
                last.then_inc(full["P3a"], 1)
            if X:
                pe.wait_ge(free["P2"], i * 4 + 3)
                for t in range(TT):
                    for k in range(KD):
                        last = three(pe, bank(Dn[0])[:, t, :], nT, swvs, lambda m: m[:, k, t * P:(t + 1) * P],
                                     lambda m: m[:, k, :], k == 0, k == KD - 1)
                last.then_inc(full["P2"], 1)

        def pe_P3b(pe, b, part):
            if part == 0:
                wait_dense(pe, "P3b", b)
                pe.wait_ge(ln_done["n2"], b + 1)
                pe_transpose_in(pe, n2, Dn[0]).then_inc(t2_full, 1)
            elif part == 1:
                pe.wait_ge(h2_ready, b + 1)
                for t in range(TT):
                    for k in range(KD):
                        last = pe.matmul(Dn[1][:, t * E:(t + 1) * E], tf[:, k, t * P:(t + 1) * P], wrs[:, k, :],
                                         start=k == 0, stop=k == KD - 1)
                last.then_inc(full["P3b"], 1)
            else:
                pe.wait_ge(masks_ready, b + 1)
                pe.wait_ge(macc_ready, b + 1)
                mm = [M[:, t, :, :].rearrange("p a e -> p (a e)") for t in range(TT)]
                pe.matmul(Dn[0][:, 0:16], upper[:, :], mm[0], start=True, stop=False)
                pe.matmul(Dn[0][:, 0:16], ones_b[:, :], macc[:, :], start=False, stop=True)
                pe.matmul(Dn[0][:, 16:32], upper[:, :], mm[1], start=True, stop=False)
                pe.matmul(Dn[0][:, 16:32], ones_b[:, :], mm[0], start=False, stop=False)
                last = pe.matmul(Dn[0][:, 16:32], ones_b[:, :], macc[:, :], start=False, stop=True)
                last.then_inc(full["P3b"], 1)

        cnt_full, idsT_full = sem("cnt_full"), sem("idsT_full")
        xt_hi, pool_link, vx_ones, pool_b2, ld_tab2 = (sem(n) for n in (
            "xt_hi", "pool_link", "vx_ones", "pool_b2", "ld_tab2"))
        ld_b1, ld_b2 = [sem(f"ld_b1_{k}") for k in range(2)], [sem(f"ld_b2_{k}") for k in range(2)]
        cx_full, m1_full, m2_full = sem("cx_full"), sem("m1_full"), sem("m2_full")
        xt_ready, relu_done, h_hi, h_ready, y_ready = (sem(n) for n in ("xt_ready", "relu_done", "h_hi", "h_ready", "y_ready"))
        xtf_ready = sem("xtf_ready")
        gath = [[sem(f"gathered{k}_{q}") for q in range(2)] for k in range(2)]
        gi_ready = sem("gi_ready")
        ld_w1, ld_w2 = sem("ld_w1"), sem("ld_w2")
        we_hi, we_lo = sem("we_hi"), sem("we_lo")
        st_y = [sem(f"st_y{k}") for k in range(2)]
        b_link, ids_sel, ids_ready, pool_b = sem("b_link"), sem("ids_sel"), sem("ids_ready"), sem("pool_b")
        ld_route, ld_tab = sem("ld_route"), sem("ld_tab")
        exb_in, exb = sem("exb_in"), sem("exb")
        gates_ready = sem("gates_ready")
        phase_a_done = sem("phase_a_done")
        rows_gathered = [sem(f"rows_gathered{k}") for k in range(UD)]
        ld_base, st_out = [sem(f"ld_base{k}") for k in range(2)], [sem(f"st_out{k}") for k in range(2)]
        comb_mid, comb = sem("comb_mid"), sem("comb")

        NG = E * C // 256
        TB, MB, YB = Sp[0], [Sp[1], Sn[0], Sn[1], Op[0]], [Op[1], Dn[0]]

        def groups(eng, body):
            body(0)
            with eng.Fori(1, NG // 8 - 1) as j:
                body(j)
            body(NG // 8 - 1)

        def c_T(pe, j, k):
            g, r = j * 8 + k, k % 2
            n = j * 4 + k // 2
            for q in range(2):
                pe.wait_ge(gath[r][q], n * 16 + 16)
            if not (first(j) and k == 0):
                pe.wait_ge(xtf_ready, g)
            for q in range(2):
                for d in range(KD):
                    last = pe.transpose(bank(TB)[:, d, q * P:(q + 1) * P], Xg[r][:, q, d * P:(d + 1) * P], ident[:, :])
            last.then_inc(cx_full, 1)

        def c_M1(pe, j, k):
            g, e2 = j * 8 + k, k // 4
            if k % 4 == 0:
                pe.wait_ge(we_lo, (j * 2 + e2 + 1) * 2)
            pe.wait_ge(xt_ready, g + 1)
            for c in range(4):
                if not (first(j) and k == 0):
                    pe.wait_ge(relu_done, g * 4 + c - 3)
                for i2 in range(2):
                    f = 2 * c + i2
                    for d in range(KD):
                        last = three(pe, bank(MB[c])[:, i2, :], W1[e2], XT[k % 2], lambda m: m[:, d, f * P:(f + 1) * P],
                                     lambda m: m[:, d, :], d == 0, d == KD - 1)
                last.then_inc(m1_full, 1)

        def c_M2(pe, j, k):
            g, e2, r = j * 8 + k, (k // 4) % 2, k % 2
            pe.wait_ge(h_ready, g * 4 + 4)
            if not (first(j) and k < 2):
                pe.wait_ge(y_ready, g - 1)
            for q in range(2):
                for f in range(FT):
                    last = three(pe, bank(YB[r])[:, q, :], HT_[r], W2[e2], lambda m: m[:, f, q * P:(q + 1) * P],
                                 lambda m: m[:, f, :], f == 0, f == FT - 1)
            last.then_inc(m2_full, 1)

        @blk.tensor
        def _(pe):
            pe.wait_ge(consts, 1)
            pe_P1(pe, 0, range(14))
            for h in range(H):
                pe_X1(pe, 0, h)
            pe_neg(pe, 0, x1_max, negx_full)

            def body(i):
                X, Y, Z, W = has(i), has(i - 1), has(i + 1), has(i - 2)
                for h in range(STEPS_A):
                    if X and h < H:
                        pe_X2(pe, i, h)
                    if Y and h >= LAG:
                        pe_Y1(pe, i - 1, h - LAG)
                    if X and 1 <= h <= H:
                        pe_XAV(pe, i, h - 1)
                    if Z:
                        pe_P1(pe, i + 1, P1_AT.get(h, ()))
                if Y:
                    pe_neg(pe, i - 1, y1_max, negy_full)
                if Z:
                    pe_P1(pe, i + 1, P1_LAST)
                if first(i):
                    pe.wait_ge(w_lo, 8)
                for h in range(STEPS_C):
                    if Y and h < H:
                        pe_Y2(pe, i - 1, h)
                    if Z and h < H:
                        pe_X1(pe, i + 1, h)
                    if Y and 1 <= h <= H:
                        pe_YAV(pe, i - 1, h - 1)
                    if Y and h >= 5 and h % 4 == 1:
                        pe_YT(pe, i - 1, h // 4 - 1)
                    if X and h in XO_AT:
                        pe_XO(pe, i, XO_AT.index(h))
                    if W and h in P3B_AT:
                        pe_P3b(pe, i - 2, P3B_AT.index(h))
                pe_P2_P3a(pe, i, X, Y, Z)

            iterations(pe, body)
            pe.wait_ge(macc_ready, B + 1)
            pe.matmul(Dn[1][:, 0:16], ones_b[:, :], macc[:, :], start=True, stop=True).then_inc(cnt_full, 1)
            pe.wait_ge(ids_sel, 1)
            pe.transpose(Dn[0][:, 0:NI], tabf[:, 0, :], ident[0:NI, 0:NI]).then_inc(idsT_full, 1)
            c_T(pe, 0, 0)

            def body_c(j):
                for k in range(8):
                    if k < 7 or not (isinstance(j, int) and j == NG // 8 - 1):
                        c_T(pe, j, k + 1) if k < 7 else c_T(pe, j + 1, 0)
                    c_M1(pe, j, k)
                    if k or not first(j):
                        c_M2(pe, j, k - 1)

            groups(pe, body_c)
            c_M2(pe, NG // 8 - 1, 7)

        @blk.scalar
        def _(act):
            def split_hi(tensors):
                for n in tensors:
                    act.wait_ge(ld_w[n], 16)
                    for src, h, _ in weight_parts[n][1]:
                        last = act.activation(h, src, ACT.Copy)
                    last.then_inc(w_hi, 1)

            def P1(b, jobs):
                for job in jobs:
                    if job not in P1_HI:
                        continue
                    act.wait_ge(full["P1"], b * 14 + job + 1)
                    kind, n = P1_JOBS[job][:2]
                    if kind == "T":
                        if not first(b, 2):
                            act.wait_ge(qk_stored[n], (b - 1) * 96)
                        act.activation((zT, cT)[n][0], bank(Dn[n]), ACT.Copy).then_inc(hi["P1"], 1)
                    else:
                        dst, bias = (QT, bqc) if kind == "q" else (KT, bkc)
                        for j in range(2):
                            last = act.activation(dst[0][:, 2 * n + j, :], bank(Dn[job % 2])[:, j, :], ACT.Identity,
                                                  bias=bias[:, 2 * n + j:2 * n + j + 1])
                        last.then_inc(hi["P1"], 1)

            def neg(b, f, dst, s):
                act.wait_ge(f, b + 1)
                act.activation(dst[:, :], Sn[0][:, 0:S], ACT.Copy).then_inc(s, 1)

            def expo(b, h, f, s, scale, av, prev):
                act.wait_ge(f, b * H + h + 1)
                if h >= 4:
                    act.wait_ge(av, b * H + h - 3)
                elif h == 0 and prev is not None:
                    act.wait_ge(*prev)
                act.activation(PT[:, h % 4, :], Sp[h % 2][:, :], ACT.Exp, scale=scale).then_inc(s, 1)

            def y_out_T(b, g):
                act.wait_ge(y2_av, b * H + 4 * g + 4)
                if not (first(b) and g < 2):
                    act.wait_ge(oyt_full, b * GY + g - 1)
                act.activation(OY[:, g % 2, :], Op[g % 2][:, 0:S], ACT.Copy).then_inc(oy_out, 1)

            def P3b(b):
                act.wait_ge(t2_full, b + 1)
                for k in range(KD):
                    last = act.activation(tf[:, k, :], bank(Dn[0])[:, k, :], ACT.Identity, scale=g2c[:, k:k + 1],
                                          bias=b2c[:, k:k + 1])
                last.then_inc(h2_ready, 1)

            def XO(b, step):
                act.wait_ge(full["XO"], b * 6 + step + 1)
                act.activation(OT[0][:, 2 * step:2 * step + 2, :], bank(Dn[step % 2]), ACT.Copy).then_inc(hi["XO"], 1)

            def P2(b):
                act.wait_ge(full["P2"], b * 4 + 1)
                for k in range(KD):
                    last = act.activation(tf[:, k, :], bank(Dn[0])[:, k, :], ACT.Identity, scale=g1c[:, k:k + 1],
                                          bias=b1c[:, k:k + 1])
                last.then_inc(tf_ready, 1)

            def P2_hi(b):
                act.wait_ge(tf_ready, b + 1)
                act.activation(nT[0], tf[:, :, :], ACT.Copy).then_inc(hi["P2"], 1)

            def P2_qk(b):
                for job, parts, bias in ((1, q_parts, sbqc), (2, k_parts, sbkc)):
                    act.wait_ge(full["P2"], b * 4 + job + 1)
                    for j in range(2):
                        last = act.activation(parts[0][:, j, :], bank(Dn[job % 2])[:, j, :], ACT.Identity,
                                              bias=bias[:, j:j + 1])
                    last.then_inc(hi["P2"], 1)

            def P3a(b):
                act.wait_ge(full["P3a"], b * 2 + 1)
                act.activation(O2T[0], bank(Dn[1]), ACT.Copy).then_inc(hi["P3a"], 1)

            split_hi(range(3))
            act.wait_ge(ld_small, 16 * SMALL)
            P1(0, range(14))
            split_hi(range(3, 8))
            neg(0, negx_full, mT, negx)

            def body(i):
                X, Y, Z, W = has(i), has(i - 1), has(i + 1), has(i - 2)
                for h in range(STEPS_A):
                    if X and h < H:
                        prev = None if first(i) else (x2_av, H) if first(i, 2) else (y2_av, (i - 1) * H)
                        expo(i, h, x2_full, x2_exp, XS, x2_av, prev)
                    if Z:
                        P1(i + 1, P1_AT.get(h, ()))
                if Y:
                    neg(i - 1, negy_full, mT, negy)
                for h in range(STEPS_C):
                    if Y and h < H:
                        expo(i - 1, h, y2_full, y2_exp, YS, y2_av, (x2_av, (i + 1) * H) if X else (y2_av, (i - 1) * H))
                    if Y and h >= 4 and h % 4 == 0:
                        y_out_T(i - 1, h // 4 - 1)
                    if X and h in XO_AT[:4]:
                        XO(i, XO_AT.index(h))
                    if W and h == P3B_AT[0]:
                        P3b(i - 2)
                if X:
                    P2(i)
                if Z:
                    neg(i + 1, negx_full, mT, negx)
                if X:
                    P2_hi(i)
                if Y:
                    P3a(i - 1)
                if X:
                    P2_qk(i)

            iterations(act, body)

            def weights(e, e2):
                act.wait_ge(ld_w1, e * 16 + 16)
                if not first(e, 2):
                    act.wait_ge(m1_full, (e - 1) * 16)
                act.activation(W1[e2][0][:, :, :], w1s[:, :, :], ACT.Copy).then_inc(we_hi, 1)
                act.wait_ge(ld_w2, e * 16 + 16)
                if not first(e, 2):
                    act.wait_ge(m2_full, (e - 1) * 4)
                act.activation(W2[e2][0][:, :, :], w2s[:, :, :], ACT.Copy).then_inc(we_hi, 1)

            def xtf(j, k):
                g = j * 8 + k
                act.wait_ge(cx_full, g + 1)
                if not (first(j) and k == 0):
                    act.wait_ge(xt_ready, g)
                for d in range(KD):
                    last = act.activation(XTf[:, d, :], bank(TB)[:, d, :], ACT.Identity, scale=g2c[:, d:d + 1],
                                          bias=b2c[:, d:d + 1])
                last.then_inc(xtf_ready, 1)

            def relu(j, k):
                g = j * 8 + k
                if k % 4 == 0:
                    act.wait_ge(ld_b1[k // 4], j * 16 + 16)
                for c in range(5):
                    if c < 4:
                        act.wait_ge(m1_full, g * 4 + c + 1)
                        if not (first(j) and k == 0 and c < 2):
                            act.wait_ge(h_ready, g * 4 + c - 1)
                        for i2 in range(2):
                            last = act.activation(hid[c % 2][:, i2, :], bank(MB[c])[:, i2, :], ACT.Relu,
                                                  bias=b1e[k // 4][:, 2 * c + i2:2 * c + i2 + 1])
                        last.then_inc(relu_done, 1)
                    if c:
                        act.wait_ge(relu_done, g * 4 + c)
                        if c == 1 and not (first(j) and k < 2):
                            act.wait_ge(m2_full, g - 1)
                        act.activation(HT_[k % 2][0][:, 2 * c - 2:2 * c, :], hid[(c - 1) % 2][:, :, :],
                                       ACT.Copy).then_inc(h_hi, 1)

            act.wait_ge(ids_ready, 1)
            weights(0, 0)
            xtf(0, 0)
            act.wait_ge(exb_in, 1)
            act.activation(ex[:, :, :], ex[:, :, :], ACT.Exp).then_inc(exb, 1)
            act.wait_ge(exb_in, 2)
            act.activation(bb[2][:, :], bb[2][:, :], ACT.Exp).then_inc(exb, 1)

            def body_c(j):
                for k in range(8):
                    if k % 4 == 1 and not (k == 5 and isinstance(j, int) and j == NG // 8 - 1):
                        weights(j * 2 + k // 4 + 1, 1 - k // 4)
                    if k < 7 or not (isinstance(j, int) and j == NG // 8 - 1):
                        xtf(j, k + 1) if k < 7 else xtf(j + 1, 0)
                    relu(j, k)

            groups(act, body_c)


        @blk.vector
        def _(dve):
            def f32(ap):
                return ap.bitcast(F32)

            dve.wait_ge(pool_consts, 1)
            dve.tensor_tensor(pick_x[:, :], ident[:, 0:HT], ident[:, 64:64 + HT], ALU.add).then_inc(consts, 1)

            def split_lo(tensors):
                for n in tensors:
                    dve.wait_ge(w_hi, n + 1)
                    for src, h, low in weight_parts[n][1]:
                        last = dve.tensor_tensor(low, src, f32(h), ALU.subtract)
                    last.then_inc(w_lo, 1)

            def ln_stats(n, src, b):
                st, mv, _ = stats[n]
                for t in range(TT):
                    last = dve.bn_stats(st[:, t, :], src[:, t, :])
                last.then_inc(bn_link[n], 1)
                hold(dve, bn_link[n], b + 1)
                for t in range(TT):
                    last = dve.bn_aggr(mv[:, t, :], st[:, t, :])
                last.then_inc(mv_done[n], 1)

            def ln_apply(n, src, dst, b):
                _, mv, rs = stats[n]
                dve.wait_ge(rs_done[n], b + 1)
                for t in range(TT):
                    last = dve.tensor_scalar(dst[:, t, :], src[:, t, :], mv[:, t, 0:1], rs[:, t:t + 1],
                                             ALU.subtract, ALU.mult)
                last.then_inc(ln_done[n], 1)

            def lnx_stats(b):
                dve.wait_ge(ld_x, b * 16 + 16)
                ln_stats("x", xt, b)

            def P1(b, jobs):
                for job in jobs:
                    d = Dn[job % 2]
                    if job in P1_HI:
                        dve.wait_ge(hi["P1"], b * 10 + P1_HI.index(job) + 1)
                    else:
                        dve.wait_ge(full["P1"], b * 14 + job + 1)
                    kind, n = P1_JOBS[job][:2]
                    if kind == "T":
                        m = (zT, cT)[n]
                        last = dve.tensor_tensor(m[1], bank(d), f32(m[0]), ALU.subtract)
                    elif kind in "qk":
                        dst, bias = (QT, bqc) if kind == "q" else (KT, bkc)
                        for t in (2 * n, 2 * n + 1):
                            last = dve.scalar_tensor_tensor(dst[1][:, t, :], bank(d)[:, t % 2, :], bias[:, t:t + 1],
                                                            f32(dst[0][:, t, :]), ALU.add, ALU.subtract)
                    else:
                        half = P1_JOBS[job][2]
                        last = dve.tensor_tensor(
                            Vx[:, n, half * 8:half * 8 + 8, 0:HD], d[:, :].rearrange("p (h c) -> p h c", c=HD),
                            bv_r[:, half * 512:(half + 1) * 512].rearrange("p (h c) -> p h c", c=HD), ALU.add)
                    last.then_inc(free["P1"], 1)

            def row_max(b, h, f, s, odd):
                dve.wait_ge(f, b * H + h + 1)
                dve.tensor_reduce(nm[:, :, odd * (h % 2) + h // 2], bank(Sn[h % 2]), AX_X, ALU.max, negate=True).then_inc(s, 1)

            def normalise(b, g, av, heads, groups, rc, width, dst, link, s):
                dve.wait_ge(av, b * H + heads * (g + 1))
                o = Op[g % 2][:, 0:TT * heads * (width + 1)].rearrange("p (q a c) -> p q a c", q=TT, a=heads)
                r = rc[:, g % 2, :].rearrange("p (q a) -> p q a", q=TT)
                if g >= 2 or not first(b):
                    dve.wait_ge(s, b * groups + g - 1)
                dve.reciprocal(r, o[:, :, :, width]).then_inc(link, 1)
                dve.wait_ge(link, b * groups + g + 1)
                dve.tensor_tensor(dst[:, :, g * heads * width:(g + 1) * heads * width]
                                  .rearrange("p q (a c) -> p q a c", a=heads), o[:, :, :, 0:width],
                                  r.unsqueeze(3).to_broadcast([P, TT, heads, width]), ALU.mult).then_inc(s, 1)

            def xnorm(b, g):
                normalise(b, g, x2_av, 2, GX, rcx, HD, O, rec_x, xo_norm)

            def ynorm(b, g):
                dve.wait_ge(oyt_full, b * GY + g + 1)
                o = bank(Op[g % 2])[:, 1, :].rearrange("p (q a c) -> p q a c", q=TT, a=4)
                r = rcy[:, g % 2, 0:TT * 4].rearrange("p (q a) -> p q a", q=TT)
                if g >= 2 or not first(b):
                    dve.wait_ge(yo_norm, b * GY + g - 1)
                dve.reciprocal(r, o[:, :, :, SD]).then_inc(rec_y, 1)
                dve.wait_ge(rec_y, b * GY + g + 1)
                dve.tensor_tensor(O2[:, :, g * 4 * SD:(g + 1) * 4 * SD].rearrange("p q (a c) -> p q a c", a=4),
                                  o[:, :, :, 0:SD], r.unsqueeze(3).to_broadcast([P, TT, 4, SD]),
                                  ALU.mult).then_inc(yo_norm, 1)

            def XO(b, step):
                if step < 4:
                    dve.wait_ge(hi["XO"], b * 4 + step + 1)
                    o = slice(2 * step, 2 * step + 2)
                    dve.tensor_tensor(OT[1][:, o, :], bank(Dn[step % 2]), f32(OT[0][:, o, :]),
                                      ALU.subtract).then_inc(free["XO"], 1)
                elif step % 2:
                    q = step // 2 - 2
                    dve.wait_ge(full["XO"], b * 6 + 5 + q)
                    if q == 0:
                        dve.wait_ge(xb_ready, b + 1)
                    dve.tensor_tensor(xb[:, q, :], Dn[q][:, 0:D], xb[:, q, :], ALU.add).then_inc(free["XO"], 1)

            def P2(b):
                dve.wait_ge(hi["P2"], b * 3 + 1)
                dve.tensor_tensor(nT[1], tf[:, :, :], f32(nT[0]), ALU.subtract).then_inc(free["P2"], 1)

            def P2_qk(b):
                for job, parts, bias in ((1, q_parts, sbqc), (2, k_parts, sbkc)):
                    dve.wait_ge(hi["P2"], b * 3 + job + 1)
                    for j in range(2):
                        last = dve.scalar_tensor_tensor(parts[1][:, j, :], bank(Dn[job % 2])[:, j, :],
                                                        bias[:, j:j + 1], f32(parts[0][:, j, :]),
                                                        ALU.add, ALU.subtract)
                    last.then_inc(free["P2"], 1)

            def P2_v(b):
                dve.wait_ge(full["P2"], b * 4 + 4)
                dve.tensor_tensor(Vs[:, :, :, 0:SD], Dn[0][:, :].rearrange("p (t h r) -> p t h r", t=TT, r=SD),
                                  sbv_r[:, :].rearrange("p (h r) -> p h r", r=SD).unsqueeze(1)
                                  .to_broadcast([P, TT, H, SD]), ALU.add).then_inc(free["P2"], 1)

            def P3a(b):
                dve.wait_ge(hi["P3a"], b + 1)
                dve.tensor_tensor(O2T[1], bank(Dn[1]), f32(O2T[0]), ALU.subtract).then_inc(free["P3a"], 1)

            def P3a_z1(b):
                dve.wait_ge(full["P3a"], b * 2 + 2)
                dve.wait_ge(zk_ready, b + 1)
                dve.tensor_tensor(zk[:, :, :], bank(Dn[1]), zk[:, :, :], ALU.add).then_inc(free["P3a"], 1)

            def each(ap, n=TT):
                return ap.unsqueeze(1).to_broadcast([P, n, E])

            def over(ap, n=TT):
                return ap.unsqueeze(2).to_broadcast([P, n, E])

            def router(b):
                dve.wait_ge(full["P3b"], b * 2 + 1)
                if not first(b):
                    dve.wait_ge(st_r, b * 16)
                dve.tensor_copy(R[:, :, 0:E], Dn[1][:, 0:TT * E].rearrange("p (t e) -> p t e", e=E))\
                   .then_inc(free["P3b"], 1)
                dve.wait_ge(free["P3b"], b * 2 + 1)
                link = Chain(dve, route_link, 20, b)
                L = R[:, :, 0:E]
                link(dve.tensor_reduce(R[:, :, 12], L, AX_X, ALU.max))
                link(dve.tensor_tensor(eq[:, :, :], L, over(R[:, :, 12]), ALU.is_equal))
                link(dve.tensor_tensor(m1[:, :, :], eq[:, :, :], each(desc[:, :]), ALU.mult))
                link(dve.tensor_reduce(R[:, :, 10], m1[:, :, :], AX_X, ALU.max))
                link(dve.tensor_tensor(m1[:, :, :], each(desc[:, :]), over(R[:, :, 10]), ALU.is_equal))
                link(dve.scalar_tensor_tensor(L2[:, :, :], m1[:, :, :], -3.0e38, L, ALU.mult, ALU.add))
                link(dve.tensor_reduce(R[:, :, 13], L2[:, :, :], AX_X, ALU.max))
                link(dve.tensor_tensor(eq[:, :, :], L2[:, :, :], over(R[:, :, 13]), ALU.is_equal))
                link(dve.tensor_tensor(L2[:, :, :], eq[:, :, :], each(desc[:, :]), ALU.mult))
                link(dve.tensor_reduce(R[:, :, 11], L2[:, :, :], AX_X, ALU.max))
                link(dve.tensor_copy(M[:, :, 0, :], m1[:, :, :]))
                dve.tensor_tensor(M[:, :, 1, :], each(desc[:, :]), over(R[:, :, 11]), ALU.is_equal)\
                   .then_inc(masks_ready, 1)
                return link

            def ranks(b):
                link = Chain(dve, route_link, 20, b)
                link.n = 11
                dve.wait_ge(full["P3b"], b * 2 + 2)
                dve.wait_ge(masks_ready, b + 1)
                dve.tensor_tensor(mr[:, :, :, :], Dn[0][:, 0:32].rearrange("p (t a e) -> p t a e", t=TT, a=2),
                                  M[:, :, :, :], ALU.mult).then_inc(free["P3b"], 1)
                link(dve.tensor_tensor(macc[:, :], macc[:, :], M[:, 0, :, :].rearrange("p a e -> p (a e)"), ALU.add))
                dve.tensor_tensor(macc[:, :], macc[:, :], M[:, 1, :, :].rearrange("p a e -> p (a e)"), ALU.add)\
                   .then_inc(macc_ready, 1)
                dve.wait_ge(free["P3b"], b * 2 + 2)
                link(dve.tensor_reduce(R[:, :, 8:10], mr[:, :, :, :], AX_X, ALU.add))
                link(dve.tensor_scalar(slot[:, :, :], R[:, :, 10:12], -float(C), float(E * C), ALU.mult, ALU.add))
                link(dve.tensor_tensor(slot[:, :, 0], slot[:, :, 0], R[:, :, 8], ALU.add))
                link(dve.scalar_tensor_tensor(slot[:, :, 1], slot[:, :, 1], float(C - 1), R[:, :, 9],
                                              ALU.add, ALU.subtract))
                link(dve.tensor_scalar(oob[:, :, :], R[:, :, 8:10], float(C), FAR, ALU.is_ge, ALU.mult))
                link(dve.tensor_tensor(slot[:, :, :], slot[:, :, :], oob[:, :, :], ALU.add))
                if not first(b):
                    dve.wait_ge(scattered, b * 64)
                link(dve.tensor_copy(tok_i[:, :], tok_f[:, :]))
                link(dve.tensor_scalar(tok_f[:, :], tok_f[:, :], float(S), None, ALU.add))
                dve.tensor_copy(slot_u[:, :, :], slot[:, :, :]).then_inc(slots_ready, 1)
                link.done()

            lnx_stats(0)
            ln_apply("x", xt, tn, 0)
            split_lo(range(3))
            dve.wait_ge(ld_small, 16 * SMALL)
            P1(0, range(14))
            for s in zeroed:
                dve.wait_ge(s, 16)
            for h in range(H):
                row_max(0, h, x1_full, x1_max, P // 2)
            split_lo(range(3, 8))

            def body(i):
                X, Y, Z, W = has(i), has(i - 1), has(i + 1), has(i - 2)
                for h in range(STEPS_A):
                    if Z and h == 0:
                        lnx_stats(i + 1)
                    if W and h == 1:
                        dve.wait_ge(free["P3a"], (i - 1) * 2)
                        ln_stats("n2", zk, i - 2)
                    if Z and h == 2:
                        ln_apply("x", xt, tn, i + 1)
                    if W and h == 3:
                        if not first(i - 2):
                            dve.wait_ge(st_n2, (i - 2) * 16)
                        ln_apply("n2", zk, n2, i - 2)
                    if Y and h >= LAG:
                        row_max(i - 1, h - LAG, y1_full, y1_max, HT)
                    if X and 2 <= h <= H and h % 2 == 0:
                        xnorm(i, h // 2 - 1)
                    if Z:
                        P1(i + 1, P1_AT.get(h, ()))
                if Z:
                    P1(i + 1, P1_LAST)
                for h in range(STEPS_C):
                    if Z and h < H:
                        row_max(i + 1, h, x1_full, x1_max, P // 2)
                    if X and h in XO_AT:
                        XO(i, XO_AT.index(h))
                    if X and h == XO_AT[7] + 1:
                        dve.wait_ge(free["XO"], i * 6 + 6)
                        ln_stats("z", xb, i)
                    if X and h == XO_AT[7] + 2:
                        if not first(i):
                            dve.wait_ge(zk_ready, i)
                            dve.wait_ge(xk_ready, i)
                        ln_apply("z", xb, z, i)
                    if X and h == XO_AT[7] + 3:
                        dve.wait_ge(ln_done["z"], i + 1)
                        ln_stats("n1", z, i)
                    if Y and h >= 6 and h % 4 == 2:
                        ynorm(i - 1, h // 4 - 1)
                    if W and h == P3B_AT[1] + 1:
                        router(i - 2)
                    if X and h == XO_AT[7] + 5:
                        ln_apply("n1", z, tn, i)
                    if W and h == P3B_AT[2]:
                        ranks(i - 2)
                if X:
                    P2(i)
                if Y:
                    P3a(i - 1)
                if X:
                    P2_qk(i)
                if Y:
                    P3a_z1(i - 1)
                if X:
                    P2_v(i)

            iterations(dve, body)

            link = Chain(dve, b_link, 27, 0)
            dve.wait_ge(ld_tab, 16)
            dve.wait_ge(ld_tab2, 16)
            dve.wait_ge(pool_b, 3)
            dve.wait_ge(cnt_full, 1)
            link(dve.tensor_copy(cnt[:, :], Dn[1][:, 0:16]))
            link(dve.tensor_copy(tabf[:, :, :], tabs[:, :, :]))
            link(dve.tensor_scalar(spos_i[:, :], spos_i[:, :], C - 1, None, ALU.bitwise_and))
            link(dve.tensor_copy(spos[:, :], spos_i[:, :]))
            link(dve.tensor_tensor(own_e[:, :], own_e[:, :], cnt[0:NI, 0:E], ALU.mult))
            link(dve.tensor_reduce(cnt_own[:, :], own_e[:, :], AX_X, ALU.add))
            link(dve.tensor_scalar(spos[:, :], spos[:, :], cnt_own[:, 0:1], None, ALU.is_lt))
            link(dve.tensor_tensor(tabf[:, 0, :], tabf[:, 0, :], tabf[:, 1, :], ALU.subtract))
            link(dve.tensor_tensor(tabf[:, 0, :], tabf[:, 0, :], spos[:, :], ALU.mult))
            dve.tensor_tensor(tabf[:, 0, :], tabf[:, 0, :], tabf[:, 1, :], ALU.add).then_inc(ids_sel, 1)
            dve.wait_ge(idsT_full, 1)
            dve.tensor_copy(ids_u[:, :], Dn[0][:, 0:NI]).then_inc(ids_ready, 1)

            def gates():
                dve.wait_ge(ld_route, 16)
                Rv = Ra[:, :, :, :].rearrange("p b t c -> p (b t) c")
                r1, r2, f1, f2, v1, v2 = (Rv[:, :, c] for c in range(8, 14))
                dve.tensor_tensor(ex[:, :, :], Rv[:, :, 0:E], over(v1, NT), ALU.subtract).then_inc(exb_in, 1)
                dve.tensor_tensor(bb[2][:, :], v2, v1, ALU.subtract).then_inc(exb_in, 1)
                dve.wait_ge(exb, 2)
                link(dve.tensor_reduce(bb[0][:, :], ex[:, :, :], AX_X, ALU.add))
                link(dve.reciprocal(bb[1][:, :], bb[0][:, :]))
                link(dve.tensor_tensor(bb[2][:, :], bb[2][:, :], bb[1][:, :], ALU.mult))
                link(dve.tensor_tensor(ex[:, :, :], each(desc[:, :], NT), over(f2, NT), ALU.is_equal))
                link(dve.tensor_tensor(ex[:, :, :], ex[:, :, :], each(cnt[:, 0:E], NT), ALU.mult))
                link(dve.tensor_reduce(bb[3][:, :], ex[:, :, :], AX_X, ALU.add))
                link(dve.tensor_tensor(bb[3][:, :], bb[3][:, :], r2, ALU.add))
                link(dve.scalar_tensor_tensor(bb[4][:, :], r1, float(C), bb[1][:, :], ALU.is_lt, ALU.mult))
                link(dve.scalar_tensor_tensor(bb[5][:, :], bb[3][:, :], float(C), bb[2][:, :], ALU.is_lt, ALU.mult))
                link(dve.tensor_tensor(bb[6][:, :], bb[4][:, :], bb[5][:, :], ALU.add))
                link(dve.tensor_scalar(bb[6][:, :], bb[6][:, :], FLT_EPS, None, ALU.max))
                link(dve.reciprocal(bb[7][:, :], bb[6][:, :]))
                link(dve.scalar_tensor_tensor(gate[0][:, :], bb[4][:, :], KEEP, bb[7][:, :], ALU.mult, ALU.mult))
                link(dve.scalar_tensor_tensor(gate[1][:, :], bb[5][:, :], KEEP, bb[7][:, :], ALU.mult, ALU.mult))
                link(dve.tensor_scalar(bb[8][:, :], r1, float(C - 1), float(E * C), ALU.min, ALU.add))
                link(dve.scalar_tensor_tensor(bb[8][:, :], f1, -float(C), bb[8][:, :], ALU.mult, ALU.add))
                link(dve.tensor_copy(gidx[0][:, :], bb[8][:, :]))
                link(dve.tensor_scalar(bb[0][:, :], r2, float(C - 1), float(E * C + C - 1), ALU.min, ALU.subtract))
                link(dve.scalar_tensor_tensor(bb[0][:, :], f2, float(C), bb[0][:, :], ALU.mult, ALU.add))
                dve.tensor_scalar(gidx[1][:, :], bb[0][:, :], -1.0, None, ALU.mult).then_inc(gates_ready, 1)
                link.per = link.n
                link.done()

            def weights(e, e2):
                dve.wait_ge(we_hi, e * 2 + 1)
                dve.tensor_tensor(W1[e2][1][:, :, :], w1s[:, :, :], f32(W1[e2][0][:, :, :]),
                                  ALU.subtract).then_inc(we_lo, 1)
                dve.wait_ge(we_hi, e * 2 + 2)
                dve.tensor_tensor(W2[e2][1][:, :, :], w2s[:, :, :], f32(W2[e2][0][:, :, :]),
                                  ALU.subtract).then_inc(we_lo, 1)

            def xt_split(j, k):
                g, r = j * 8 + k, k % 2
                dve.wait_ge(xtf_ready, g + 1)
                if not (first(j) and k < 2):
                    dve.wait_ge(m1_full, (g - 1) * 4)
                dve.tensor_copy(XT[r][0][:, :, :], XTf[:, :, :]).then_inc(xt_hi, 1)
                dve.wait_ge(xt_hi, g + 1)
                dve.tensor_tensor(XT[r][1][:, :, :], XTf[:, :, :], f32(XT[r][0][:, :, :]),
                                  ALU.subtract).then_inc(xt_ready, 1)

            def hid_lo(j, k):
                g = j * 8 + k
                for c in range(4):
                    dve.wait_ge(h_hi, g * 4 + c + 1)
                    o = slice(2 * c, 2 * c + 2)
                    dve.tensor_tensor(HT_[k % 2][1][:, o, :], hid[c % 2][:, :, :], f32(HT_[k % 2][0][:, o, :]),
                                      ALU.subtract).then_inc(h_ready, 1)

            def y_out(j, k):
                g, r, e2 = j * 8 + k, k % 2, (k // 4) % 2
                dve.wait_ge(m2_full, g + 1)
                if not (first(j) and k < 2):
                    dve.wait_ge(st_y[r], (j * 4 + (k - r) // 2) * 16)
                if k % 4 == 0:
                    dve.wait_ge(ld_b2[e2], (j + (k // 8)) * 16 + 16)
                dve.tensor_tensor(ys[r][:, :, :], bank(YB[r]), b2e[e2][:, :].unsqueeze(1).to_broadcast([P, 2, D]),
                                  ALU.add).then_inc(y_ready, 1)

            weights(0, 0)
            xt_split(0, 0)
            gates()

            def body_c(j):
                for k in range(8):
                    if k % 4 == 1 and not (k == 5 and isinstance(j, int) and j == NG // 8 - 1):
                        weights(j * 2 + k // 4 + 1, 1 - k // 4)
                    if k < 7 or not (isinstance(j, int) and j == NG // 8 - 1):
                        xt_split(j, k + 1) if k < 7 else xt_split(j + 1, 0)
                    hid_lo(j, k)
                    if k or not first(j):
                        y_out(j, k - 1)

            groups(dve, body_c)
            y_out(NG // 8 - 1, 7)

            for n in range(NT // UD):
                dve.wait_ge(ld_base[n % 2], 16 * (n // 2 + 1))
                for k in range(UD):
                    dve.wait_ge(rows_gathered[k], 32 * (n + 1))
                    c = n * UD + k
                    for j in range(2):
                        if j:
                            dve.wait_ge(comb_mid, c + 1)
                        dve.scalar_tensor_tensor(ba[n % 2][:, k, :], ya[j][n % 2][:, k, :], gate[j][:, c:c + 1],
                                                 ba[n % 2][:, k, :], ALU.mult, ALU.add)\
                           .then_inc((comb_mid, comb)[j], 1)

        @blk.gpsimd
        def _(pool):
            n = [0]

            def link(ins):
                n[0] += 1
                ins.then_inc(pool_link, 1)
                hold(pool, pool_link, n[0])

            link(pool.memset(ident[:, :], 0.0))
            link(pool.affine_select(out=ident[:, :], in_=ident[:, :], compare_op=ALU.not_equal, fill=1.0, base=0,
                                    pattern=[[-1, P]], channel_multiplier=1))
            link(pool.memset(upper[:, :], 1.0))
            link(pool.affine_select(out=upper[:, :], in_=upper[:, :], compare_op=ALU.is_gt, fill=0.0, base=0,
                                    pattern=[[1, P]], channel_multiplier=-1))
            link(pool.memset(ones_b[:, :], 1.0))
            pool.memset(macc[:, :], 0.0).then_inc(macc_ready, 1)
            link(pool.memset(neghalf[:, :], -0.5))
            link(pool.memset(Vs[:, :, :, :], 1.0))
            link(pool.memset(R[:, :, :], 0.0))
            few = nm[:, 0, 0:E].bitcast(I32)
            link(pool.iota(few, pattern=[[-1, E]], base=E, channel_multiplier=0))
            link(pool.tensor_copy(desc[:, :], few))
            link(pool.memset(nm[:, :, :], 0.0))
            link(pool.iota(tok_i[:, :], pattern=[[P, TT]], base=0, channel_multiplier=1))
            link(pool.tensor_copy(tok_f[:, :], tok_i[:, :]))
            for s in range(2):
                link(pool.memset(SK[64 * s + 32:64 * s + 64, :, :].bitcast(F32), 1.0))
            pool.memset(neghalf[:, :], -0.5).then_inc(pool_consts, 1)
            hold(pool, pool_consts, 1)

            def rsqrt(name, b):
                _, mv, rs = stats[name]
                hold(pool, mv_done[name], b + 1)
                pool.tensor_scalar(rs[:, :], mv[:, :, 1], EPS, None, ALU.add).then_inc(rs_link[name], 1)
                hold(pool, rs_link[name], b + 1)
                pool.tensor_tensor(rs[:, :], rs[:, :], neghalf[:, :], ALU.pow).then_inc(rs_done[name], 1)

            def both(ap):
                return ap[:, :].unsqueeze(1).to_broadcast([P, TT, D])

            rsqrt("x", 0)
            pool.wait_ge(w_lo, 2)
            pool.memset(Vx[:, :, :, HD:HD + 1], 1.0).then_inc(vx_ones, 1)
            pool.wait_ge(ld_small, 16 * SMALL)

            def scatter(b):
                hold(pool, slots_ready, b + 1)
                if first(b):
                    for s in zeroed:
                        hold(pool, s, 16)
                for t in range(TT):
                    for a in range(2):
                        pool.indirect_dma_start(slot_d[a], bass.IndirectOffsetOnAxis(slot_u[:, t, a:a + 1], 0),
                                                tok_i[:, t:t + 1], None, bounds_check=E * C - 1,
                                                oob_is_err=False).then_inc(scattered, 16)

            def body(i):
                X, Y, Z, W = has(i), has(i - 1), has(i + 1), has(i - 2)
                if Z:
                    rsqrt("x", i + 1)
                if W:
                    rsqrt("n2", i - 2)
                if Y:
                    if W:
                        hold(pool, ln_done["n2"], i - 1)
                        hold(pool, st_base, (i - 1) * 16)
                    hold(pool, ln_done["z"], i)
                    pool.tensor_tensor(zk[:, :, :], z[:, :, :], both(sbo_r), ALU.add).then_inc(zk_ready, 1)
                    pool.tensor_copy(xk[:, :, :], xb[:, :, :]).then_inc(xk_ready, 1)
                if X:
                    hold(pool, ld_r, i * 16 + 16)
                    pool.tensor_tensor(xb[:, :, :], xb[:, :, :], both(bo_r), ALU.add).then_inc(xb_ready, 1)
                if X:
                    rsqrt("z", i)
                    rsqrt("n1", i)
                if W:
                    scatter(i - 2)
                if Y:
                    hold(pool, free["P3a"], i * 2)
                    hold(pool, xk_ready, i)
                    pool.tensor_tensor(xk[:, :, :], zk[:, :, :], xk[:, :, :], ALU.add).then_inc(base_ready, 1)

            iterations(pool, body)

            hold(pool, ld_tab, 16)
            pool.iota(spos_i[:, :], pattern=[[1, P]], base=0, channel_multiplier=P).then_inc(pool_b, 1)
            pool.memset(own_e[:, :], 1.0).then_inc(pool_b2, 1)
            hold(pool, pool_b2, 1)
            pool.affine_select(out=own_e[:, :], in_=own_e[:, :], compare_op=ALU.is_ge, fill=0.0, base=0,
                               pattern=[[-(C // P), E]], channel_multiplier=1).then_inc(pool_b2, 1)
            hold(pool, pool_b2, 2)
            pool.affine_select(out=own_e[:, :], in_=own_e[:, :], compare_op=ALU.is_ge, fill=0.0, base=C // P - 1,
                               pattern=[[C // P, E]], channel_multiplier=-1).then_inc(pool_b, 2)

            def gather(j, k):
                g, r = j * 8 + k, k % 2
                if not (first(j) and k < 2):
                    hold(pool, cx_full, g - 1)
                pool.tensor_copy(gi[r][:, :], ids_u[:, bass.ds(j * 16 + 2 * k, 2)]).then_inc(gi_ready, 1)
                hold(pool, gi_ready, g + 1)
                for q in range(2):
                    pool.indirect_dma_start(Xg[r][:, q, :], None, n2_d, bass.IndirectOffsetOnAxis(gi[r][:, q:q + 1], 0),
                                            bounds_check=T - 1, oob_is_err=False).then_inc(gath[r][q], 16)

            hold(pool, ids_ready, 1)
            gather(0, 0)
            gather(0, 1)

            def body_c(j):
                for k in range(8):
                    if k < 6:
                        gather(j, k + 2)
                    elif not (isinstance(j, int) and j == NG // 8 - 1):
                        gather(j + 1, k - 6)

            groups(pool, body_c)

            for s in st_y:
                hold(pool, s, NG // 2 * 16)
            hold(pool, gates_ready, 1)
            for n in range(NT // UD):
                for k in range(UD):
                    if n:
                        pool.wait_ge(comb, (n - 1) * UD + k + 1)
                    for j in range(2):
                        pool.indirect_dma_start(ya[j][n % 2][:, k, :], None, y_d,
                                                bass.IndirectOffsetOnAxis(gidx[j][:, n * UD + k:n * UD + k + 1], 0),
                                                bounds_check=E * C - 1, oob_is_err=False)\
                            .then_inc(rows_gathered[k], 16)

        @blk.sync
        def _(sp):
            def small(dst, src):
                sp.dma_start(dst, src, allow_slow_non_contiguous=True).then_inc(ld_small, 16)
                count[0] += 1

            count = [0]

            def rows(a, b):
                return a[b, :, :].rearrange("(t p) d -> p t d", p=P) if isinstance(b, int) else \
                    a[bass.ds(b, 1), :, :].rearrange("a (t p) d -> p (a t) d", p=P)

            def tokens(a, b):
                return rows(a.rearrange("(b s) d -> b s d", s=S), b)

            def load_x(b):
                sp.dma_start(xt[:, :, :], rows(x, b)).then_inc(ld_x, 16)

            def load_c(b):
                sp.dma_start(ct[:, :, :], rows(ctx, b)).then_inc(ld_c, 16)

            def load_r(b):
                sp.dma_start(xb[:, :, :], rows(x, b)).then_inc(ld_r, 16)

            load_x(0)
            load_c(0)
            def load_weights(tensors):
                for n in tensors:
                    if n == 7:
                        sp.wait_ge(w_lo, 1)
                    (dst, src), _ = weight_parts[n]
                    sp.dma_start(dst, src).then_inc(ld_w[n], 16)

            load_weights(range(2))
            small(bqc[:, :], bq.rearrange("(t a) d -> (a d) t", a=2))
            small(bkc[:, :], bk.rearrange("(t a) d -> (a d) t", a=2))
            small(bv_r[:, :], bv.rearrange("h d -> (h d)").partition_broadcast(P))
            small(bo_r[:, :], bo.partition_broadcast(P))
            small(sbv_r[:, :], sbv.partition_broadcast(P))
            small(sbo_r[:, :], sbo.partition_broadcast(P))
            for src, dst in ((sbq, sbqc), (sbk, sbkc)):
                small(dst[:, :], src.rearrange("(t p) -> p t", p=P))
            for src, dst in ((g1, g1c), (b1n, b1c), (g2, g2c), (b2n, b2c)):
                small(dst[:, :], src.rearrange("(k p) -> p k", p=P))
            small(wrs[:, :, :], wr.rearrange("(k p) e -> p k e", p=P))
            load_weights(range(2, 7))
            assert count[0] == SMALL, count[0]
            sp.wait_ge(pool_consts, 1)
            for a in range(2):
                sp.dma_start(slot_d[a].rearrange("(p c) a -> p (c a)", p=P), nm[:, 0, 0:E * C // P].bitcast(I32)).then_inc(zeroed[a], 16)
            load_weights([7])
            load_r(0)
            sp.wait_ge(ln_done["x"], 1)
            load_x(1)
            sp.wait_ge(full["P1"], 2)
            load_c(1)

            def place_qk(b):
                parts = ((q_parts, (0, 1, 0), free["P2"], 2), (k_parts, (0, 0, 1), free["P2"], 3))
                for n, (pt, order, s, at) in enumerate(parts):
                    sp.wait_ge(s, b * 4 + at)
                    for k in range(3):
                        for t in range(KD):
                            sp.dma_start(qk_d[n].rearrange("(t h) b r q -> t b h r q", t=KD)[t, k],
                                         pt[order[k]][:, t, :].bitcast(F32)).then_inc(qk_stored[n], 16)
                for n, dst in enumerate((SQ, SK)):
                    sp.wait_ge(qk_stored[n], b * 96 + 96)
                    for s in range(2):
                        sp.dma_start(dst[64 * s:64 * s + 3 * SD, :, :].bitcast(F32),
                                     qk_d[n].rearrange("(t s) b r q -> s (b r) t q", s=2)[s])\
                            .then_inc(qk_placed[n], 16)

            def place_shifts(b):
                sp.wait_ge(negy, b + 1)
                for s in range(2):
                    sp.dma_start(SQ[64 * s + 3 * SD:64 * s + 3 * SD + 1, :, :].bitcast(F32),
                                 mT[s * HT:(s + 1) * HT, :].bitcast(F32))\
                        .then_inc(shift_placed, 16)

            def body(i):
                X, Y, W = has(i), has(i - 1), has(i - 2)
                if W:
                    sp.wait_ge(ln_done["n2"], i - 1)
                    sp.dma_start(tokens(n2_d, i - 2), n2[:, :, :]).then_inc(st_n2, 16)
                if Y and X:
                    sp.wait_ge(xk_ready, i)
                    load_r(i)
                if has(i + 2):
                    sp.wait_ge(ln_done["x"], i + 2)
                    load_x(i + 2)
                if has(i + 2):
                    sp.wait_ge(full["P1"], (i + 1) * 14 + 2)
                    load_c(i + 2)
                if Y:
                    place_shifts(i - 1)
                if W:
                    sp.wait_ge(slots_ready, i - 1)
                    sp.dma_start(route_d[i - 2] if isinstance(i, int) else
                                 route_d[bass.ds(i - 2, 1), :, :].rearrange("a p c -> (a p) c"),
                                 R[:, :, :].rearrange("p t c -> p (t c)")).then_inc(st_r, 16)
                if X:
                    place_qk(i)
                if Y:
                    sp.wait_ge(base_ready, i)
                    sp.dma_start(tokens(base_d, i - 1), xk[:, :, :]).then_inc(st_base, 16)

            def iterations_sp():
                body(0), body(1)
                with sp.Fori(2, B - 2) as i:
                    body(i)
                body(B - 2), body(B - 1), body(B), body(B + 1)

            iterations_sp()

            for s in (st_base, st_n2, st_r):
                sp.wait_ge(s, B * 16)
            sp.wait_ge(scattered, B * 64)
            sp.wait_ge(cnt_full, 1)
            for a in range(2):
                sp.dma_start(tabs[:, a, :], slot_d[a].rearrange("(n p) a -> n (p a)", p=P)).then_inc((ld_tab, ld_tab2)[a], 16)
            sp.dma_start(Ra[:, :, :, :].rearrange("p b t c -> p b (t c)"),
                         route_d.rearrange("b p c -> p b c")).then_inc(ld_route, 16)

            def at(a, e, pattern):
                return a[bass.ds(e, 1)].rearrange(pattern, p=P) if not isinstance(e, int) else \
                    a[e:e + 1].rearrange(pattern, p=P)

            def load_expert(e, e2):
                if not first(e):
                    sp.wait_ge(we_lo, e * 2 - 1)
                sp.dma_start(w1s[:, :, :], at(w1, e, "a (k p) f -> p (a k) f")).then_inc(ld_w1, 16)
                if not first(e):
                    sp.wait_ge(we_lo, e * 2)
                sp.dma_start(w2s[:, :, :], at(w2, e, "a (f p) d -> p (a f) d")).then_inc(ld_w2, 16)
                if not first(e, 2):
                    sp.wait_ge(y_ready, (e - 1) * 4)
                sp.dma_start(b1e[e2][:, :], at(b1, e, "a (f p) -> p (a f)"), allow_slow_non_contiguous=True)\
                    .then_inc(ld_b1[e2], 16)
                sp.dma_start(b2e[e2][:, :], (b2[e] if isinstance(e, int) else
                                             b2[bass.ds(e, 1), :].rearrange("a d -> (a d)")).partition_broadcast(P))\
                    .then_inc(ld_b2[e2], 16)

            def store_y(j, k):
                g, r = j * 8 + k, k % 2
                sp.wait_ge(y_ready, g + 1)
                yv = y_d.rearrange("(g q p) d -> g p q d", q=2, p=P)
                sp.dma_start(yv[bass.ds(g, 1)].rearrange("a p q d -> p (a q) d") if not isinstance(g, int) else yv[g],
                             ys[r][:, :, :]).then_inc(st_y[r], 16)

            load_expert(0, 0)
            load_expert(1, 1)

            def body_c(j):
                for k in range(8):
                    store_y(j, k)
                    if k % 4 == 2 and not (isinstance(j, int) and j == NG // 8 - 1):
                        load_expert(j * 2 + 2 + k // 4, k // 4)

            groups(sp, body_c)

            def tiles(a, n):
                return a.rearrange("(i k p) d -> i p k d", k=UD, p=P)[n]

            def load_base(n):
                sp.dma_start(ba[n % 2][:, :, :], tiles(base_d, n)).then_inc(ld_base[n % 2], 16)

            load_base(0)
            load_base(1)
            for n in range(NT // UD):
                sp.wait_ge(comb, (n + 1) * UD)
                sp.dma_start(tiles(out.rearrange("b s d -> (b s) d"), n), ba[n % 2][:, :, :]).then_inc(st_out[n % 2], 16)
                if n + 2 < NT // UD:
                    sp.wait_ge(st_out[n % 2], 16 * (n // 2 + 1))
                    load_base(n + 2)
            for k in range(2):
                sp.wait_ge(st_out[k], 16 * (NT // UD // 2))


_INS = ['x', 'ctx_1024', 'L0_xattn_Wq', 'L0_xattn_bq', 'L0_xattn_Wk', 'L0_xattn_bk', 'L0_xattn_Wv', 'L0_xattn_bv',
        'L0_xattn_Wo', 'L0_xattn_bo', 'L0_ffn_wq', 'L0_ffn_bq', 'L0_ffn_wk', 'L0_ffn_bk', 'L0_ffn_wv', 'L0_ffn_bv',
        'L0_ffn_wo', 'L0_ffn_bo', 'L0_ffn_ln1_g', 'L0_ffn_ln1_b', 'L0_ffn_ln2_g', 'L0_ffn_ln2_b', 'L0_ffn_wr',
        'L0_ffn_w1', 'L0_ffn_b1', 'L0_ffn_w2', 'L0_ffn_b2']


def kernel(**inputs):
    import numpy as np
    import concourse.bacc as bacc
    from concourse.bass_utils import run_bass_kernel_spmd

    nc = bacc.Bacc("TRN2", target_bir_lowering=False, num_devices=1)
    arrays, args = {}, []
    for name in _INS:
        a = np.ascontiguousarray(inputs[name])
        arrays[f"in_{name}"] = a
        args.append(nc.dram_tensor(f"in_{name}", a.shape, mybir.dt.from_np(a.dtype), kind="ExternalInput").ap())
    shape = arrays["in_x"].shape
    out = nc.dram_tensor("out_rows", shape, F32, kind="ExternalOutput").ap()
    xattn_moe(nc, *args, out)
    r = run_bass_kernel_spmd(nc, [arrays], core_ids=[0])
    return r.results[0]["out_rows"]
```
